# Optimizing a Trainium2 kernel written in Bass

```python
import numpy as np
import jax
import jax.numpy as jnp

def _softmax(x, axis=-1):
    return jax.nn.softmax(x, axis=axis)

def _gelu(x):
    return jax.nn.gelu(x, approximate=True)

def _silu(x):
    return jax.nn.silu(x)

def _sigmoid(x):
    return jax.nn.sigmoid(x)

def _layernorm(x, axis=-1, eps=1e-05):
    m = jnp.mean(x, axis=axis, keepdims=True)
    v = jnp.var(x, axis=axis, keepdims=True)
    return (x - m) / jnp.sqrt(v + eps)

def _scatter_add(tgt, idx, src, axis=0):
    return tgt.at[idx].add(src)

def _segment_sum(src, seg, n):
    return jax.ops.segment_sum(src, seg, n)
kernel_name = 'mk_recurrent_d1_jaxref_r4_df7796'

def setup_inputs(seed: int=0):
    np.random.seed(seed)
    _w = jnp.asarray

    def _L0_attn_setup():
        import jax, jax.numpy as jnp
        import numpy as np
        import math
        B, S, DM = (1, 512, 1024)
        H, HKV, HD = (32, 8, 128)
        EPS = 1e-06
        NEG_INF = -1e+30

        def _alibi_slopes(n_heads: int) -> np.ndarray:
            start = 2 ** (-2 ** (-(math.log2(n_heads) - 3)))
            return np.array([start * start ** i for i in range(n_heads)], dtype=np.float32)

        def _rmsnorm(t, w):
            tf = t.astype(jnp.float32)
            inv = jax.lax.rsqrt(jnp.mean(tf * tf, axis=-1, keepdims=True) + EPS)
            return (tf * inv * w).astype(t.dtype)
        key = jax.random.key(seed)
        ks = jax.random.split(key, 5)
        std = 0.02
        return {'x': jax.random.normal(ks[0], (B, S, DM), dtype=jnp.float32), 'Wq': jax.random.normal(ks[1], (H * HD, DM), dtype=jnp.float32) * std, 'Wk': jax.random.normal(ks[2], (HKV * HD, DM), dtype=jnp.float32) * std, 'Wv': jax.random.normal(ks[3], (HKV * HD, DM), dtype=jnp.float32) * std, 'Wo': jax.random.normal(ks[4], (H * HD, DM), dtype=jnp.float32).T * (std / math.sqrt(2 * 32)), 'q_norm_w': jnp.ones((HD,), dtype=jnp.float32), 'k_norm_w': jnp.ones((HD,), dtype=jnp.float32)}
    _L0_attn_in = _L0_attn_setup()

    def _L0_ffn_setup():
        import jax, jax.numpy as jnp
        import numpy as np
        B_, S, D_IN, D_OUT = (4, 512, 1024, 1024)
        N, RANK, ALPHA = (8, 16, 32)
        SCALE = ALPHA / RANK
        key = jax.random.key(seed)
        kx, ka, kb, kw, kbias = jax.random.split(key, 5)
        x = jax.random.normal(kx, (B_, S, D_IN), dtype=jnp.float32)
        lora_A = jax.random.normal(ka, (N, RANK, D_IN), dtype=jnp.float32) * (1.0 / np.sqrt(D_IN))
        lora_B = jax.random.normal(kb, (N, D_OUT, RANK), dtype=jnp.float32) * (1.0 / np.sqrt(RANK))
        W = jax.random.normal(kw, (D_OUT, D_IN), dtype=jnp.float32) * (1.0 / np.sqrt(D_IN))
        bias = jax.random.normal(kbias, (D_OUT,), dtype=jnp.float32) * 0.01
        lora_weights = jnp.full((N,), 1.0 / N, dtype=jnp.float32)
        return {'x': x, 'lora_A': lora_A, 'lora_B': lora_B, 'W': W, 'bias': bias, 'lora_weights': lora_weights}
    _L0_ffn_in = _L0_ffn_setup()
    _d = {'L0_attn_x': _L0_attn_in['x'], 'L0_attn_Wq': _L0_attn_in['Wq'], 'L0_attn_Wk': _L0_attn_in['Wk'], 'L0_attn_Wv': _L0_attn_in['Wv'], 'L0_attn_Wo': _L0_attn_in['Wo'], 'L0_attn_q_norm_w': _L0_attn_in['q_norm_w'], 'L0_attn_k_norm_w': _L0_attn_in['k_norm_w'], 'L0_ffn_lora_A': _L0_ffn_in['lora_A'], 'L0_ffn_lora_B': _L0_ffn_in['lora_B'], 'L0_ffn_W': _L0_ffn_in['W'], 'L0_ffn_bias': _L0_ffn_in['bias'], 'L0_ffn_lora_weights': _L0_ffn_in['lora_weights']}
    _x0 = _d['L0_attn_x']
    _d['L0_attn_x'] = jax.random.normal(jax.random.fold_in(jax.random.key(seed), 1), (4, 512, 1024), dtype=_x0.dtype)
    del _x0
    return _d

def reference(L0_attn_x, L0_attn_Wq, L0_attn_Wk, L0_attn_Wv, L0_attn_Wo, L0_attn_q_norm_w, L0_attn_k_norm_w, L0_ffn_lora_A, L0_ffn_lora_B, L0_ffn_W, L0_ffn_bias, L0_ffn_lora_weights):

    def _L0_attn_ref(x, Wq, Wk, Wv, Wo, q_norm_w, k_norm_w):
        import jax, jax.numpy as jnp
        import numpy as np
        import math
        B, S, DM = (1, 512, 1024)
        H, HKV, HD = (32, 8, 128)
        EPS = 1e-06
        NEG_INF = -1e+30

        def _alibi_slopes(n_heads: int) -> np.ndarray:
            start = 2 ** (-2 ** (-(math.log2(n_heads) - 3)))
            return np.array([start * start ** i for i in range(n_heads)], dtype=np.float32)

        def _rmsnorm(t, w):
            tf = t.astype(jnp.float32)
            inv = jax.lax.rsqrt(jnp.mean(tf * tf, axis=-1, keepdims=True) + EPS)
            return (tf * inv * w).astype(t.dtype)
        b, s, _ = x.shape
        G = H // HKV
        q = (x @ Wq.T).reshape(b, s, H, HD).transpose(0, 2, 1, 3)
        k = (x @ Wk.T).reshape(b, s, HKV, HD).transpose(0, 2, 1, 3)
        v = (x @ Wv.T).reshape(b, s, HKV, HD).transpose(0, 2, 1, 3)
        q = _rmsnorm(q, q_norm_w)
        k = _rmsnorm(k, k_norm_w)
        qg = q.reshape(b, HKV, G, s, HD)
        scores = jnp.einsum('bkgqd,bksd->bkgqs', qg, k) / math.sqrt(HD)
        slopes = jnp.asarray(_alibi_slopes(H)).reshape(HKV, G)
        pos = jnp.arange(s, dtype=jnp.float32)
        rel = pos[None, :] - pos[:, None]
        bias = jnp.where(rel > 0, NEG_INF, slopes[:, :, None, None] * rel)
        attn = jax.nn.softmax(scores + bias[None], axis=-1)
        out = jnp.einsum('bkgqs,bksd->bkgqd', attn, v)
        out = out.reshape(b, H, s, HD).transpose(0, 2, 1, 3).reshape(b, s, H * HD)
        return out @ Wo.T

    def _L0_ffn_ref(x, lora_A, lora_B, W, bias, lora_weights):
        import jax, jax.numpy as jnp
        import numpy as np
        B_, S, D_IN, D_OUT = (4, 512, 1024, 1024)
        N, RANK, ALPHA = (8, 16, 32)
        SCALE = ALPHA / RANK
        h = jnp.einsum('bsd,nrd->nbsr', x, lora_A)
        coef = (SCALE * lora_weights)[:, None, None]
        lora_out = jnp.einsum('nbsr,nor->bso', h, lora_B * coef)
        base = jnp.einsum('bsd,od->bso', x, W) + bias
        return base + lora_out
    x = L0_attn_x
    xn = _layernorm(x, axis=-1)
    s = _L0_attn_ref(xn, L0_attn_Wq, L0_attn_Wk, L0_attn_Wv, L0_attn_Wo, L0_attn_q_norm_w, L0_attn_k_norm_w)
    g = _silu(_L0_ffn_ref(xn, L0_ffn_lora_A, L0_ffn_lora_B, L0_ffn_W, L0_ffn_bias, L0_ffn_lora_weights))
    x = x + s * g
    return x

_drawn_inputs = setup_inputs


def setup_inputs(seed=0):
    import zlib

    import numpy as np

    out = dict(_drawn_inputs(seed))
    spreads = {'L0_attn_q_norm_w': (1.0, 0.6),
     'L0_attn_k_norm_w': (1.0, 0.6),
     'L0_ffn_lora_weights': (0.125, 0.6)}
    factors = {'L0_ffn_bias': 186.427}
    for name, (base, spread) in spreads.items():
        noise = np.random.default_rng([zlib.crc32(name.encode()), seed]).standard_normal(out[name].shape)
        drawn = base * np.exp(spread * noise) if base else spread * noise
        out[name] = jnp.asarray(drawn.astype(out[name].dtype))
    for name, factor in factors.items():
        out[name] = (out[name] * factor).astype(out[name].dtype)
    return out
```

```python
from contextlib import ExitStack

import concourse.bass as bass
from concourse import mybir

ALU = mybir.AluOpType
ACT = mybir.ActivationFunctionType
F32 = mybir.dt.float32
F32R = mybir.dt.float32r

P = 128
BATCH, S, D = 4, 512, 1024
H, HKV, HD = 32, 8, 128
G = H // HKV
NT = S // P
NK = D // P
TILE = 1024
PW = P * NT * (NT + 1) // 2
RMS_EPS, LN_EPS = 1e-6, 1e-5
LORA_SCALE = 2.0
MASKED = -1e38

KV, Q01, Q23 = 0, 1, 2
PROJ = [[(Q23, t) for t in range(4)],
        [(KV, 0), (KV, 1), (KV, 2)],
        [(KV, 3), (Q01, 0), (Q01, 1)],
        [(Q01, 2), (Q01, 3)]]

P_AT = [P * i * (i + 1) // 2 for i in range(NT)]
PT_AT = [sum(S - P * m for m in range(k)) for k in range(NT)]

SLOT2 = 2
PO_LEAD = 8


class Pos:

    def __init__(self, eng, b, g):
        self.eng, self.b, self.kept = eng, b, {}
        self.n = b * HKV + g

    def at(self, k, c, kb=0):
        if (k, kb) not in self.kept:
            v = self.n * k + self.b * kb if kb else self.n * k
            self.kept[k, kb] = self.eng.snap(v)
        return self.kept[k, kb] + c

    def po(self, c):
        return self.at(16, c, 8)

    def tb(self, c):
        return self.at(21, c + 10, 8)


def build_layer(nc, x_tok, x_last, xT, wa, wo, wT, lora_a, lora_bt, lw, ffn_b, qw, kw, rel, slopes,
                ident, outT):
    with ExitStack() as ctx:
        def sb(name, shape, dt=F32):
            return ctx.enter_context(nc.sbuf_tensor(name, shape, dt))

        def ps(name):
            return ctx.enter_context(nc.psum_tensor(name, [P, 512], F32))

        def sem(name):
            return ctx.enter_context(nc.semaphore(name))

        weff = nc.dram_tensor("weff", [NK, P, TILE], F32).ap()
        gate_dram = nc.dram_tensor("gate_dram", [NK, P, S], F32).ap()

        xtok = sb("xtok", [P, NT, D])
        xn_hi, xn_lo = sb("xn_hi", [P, NK, S], F32R), sb("xn_lo", [P, NK, S], F32R)
        acc = sb("acc", [P, NK, S])
        stage_a, stage_b = sb("stage_a", [P, 2, TILE]), sb("stage_b", [P, 2, TILE])
        wa_hi, wa_lo = sb("wa_hi", [P, 2, 2 * TILE], F32R), sb("wa_lo", [P, 2, 2 * TILE], F32R)
        wb_hi, wb_lo = sb("wb_hi", [P, 2, TILE], F32R), sb("wb_lo", [P, 2, TILE], F32R)
        raw = [sb("kv_raw", [P, NT, 256]), sb("q01_raw", [P, NT, 256]), sb("q23_raw", [P, NT, 256])]
        qT_hi, qT_lo = sb("qT_hi", [P, 2, S], F32R), sb("qT_lo", [P, 2, S], F32R)
        kT_hi, kT_lo = sb("kT_hi", [P, S], F32R), sb("kT_lo", [P, S], F32R)
        v_hi, v_lo = sb("v_hi", [P, NT, HD], F32R), sb("v_lo", [P, NT, HD], F32R)
        prob = sb("prob", [P, PW])
        pT_hi, pT_lo = sb("pT_hi", [P, PW], F32R), sb("pT_lo", [P, PW], F32R)
        bias_sb = sb("bias_sb", [P, 2, S])
        o_hi, o_lo = sb("o_hi", [P, 2, 2, S], F32R), sb("o_lo", [P, 2, 2, S], F32R)
        g_buf, x_buf = sb("g_buf", [P, 2, S]), sb("x_buf", [P, 2, S])
        ident_sb, rel_sb = sb("ident_sb", [P, P]), sb("rel_sb", [P, S])
        slope0, slope = sb("slope0", [P, G]), sb("slope", [P, G])
        qw_sb, kw_sb, qkw = sb("qw_sb", [P, 1]), sb("kw_sb", [P, 1]), sb("qkw", [P, 1])
        fb, nfb, lw_sb = sb("fb", [P, NK]), sb("nfb", [P, NK]), sb("lw_sb", [P, 1])
        sq = sb("sq", [P, 8, HD])
        ss, var, rinv, tmp = (sb(n, [P, 8]) for n in ("ss", "var", "rinv", "tmp"))
        lnv = sb("lnv", [P, 8])
        negmax, rowsum, rs_inv = (sb(n, [P, NT]) for n in ("negmax", "rowsum", "rs_inv"))
        bn = sb("bn", [P, NT, 12])
        mv = sb("mv", [P, NT, 2])

        proj_ps = [ps("proj0"), ps("proj1")]
        sc_ps = [ps("sc0"), ps("sc1")]
        tr_ps = [ps("tr0"), ps("tr1")]
        ot_ps = ps("ot")

        const_in = sem("const_in")
        x_in = sem("x_in")
        a_in = [sem("a_in0"), sem("a_in1")]
        b_in = [sem("b_in0"), sem("b_in1")]
        lora_in = sem("lora_in")
        wt_in = [sem(f"wt_in{i}") for i in range(4)]
        weff_out = [sem(f"weff_out{i}") for i in range(4)]
        gate_out = [sem("gate_out0"), sem("gate_out1")]
        fin_in = [sem("fin_in0"), sem("fin_in1")]
        res_out = [sem("res_out0"), sem("res_out1")]
        a_done = sem("a_done")
        po_done = sem("po_done")
        s_done = sem("s_done")
        tr_done = sem("tr_done")
        pv_done = sem("pv_done")
        weff_done = sem("weff_done")
        a_free = sem("a_free")
        wa_hi_done, wb_hi_done = sem("wa_hi_done"), sem("wb_hi_done")
        exp_done = sem("exp_done")
        tr_hi = sem("tr_hi")
        ot_hi = sem("ot_hi")
        v_hi_done = sem("v_hi_done")
        ln_done, r0_done = sem("ln_done"), sem("r0_done")
        gate_exp = sem("gate_exp")
        lora_hi = sem("lora_hi")
        wa_ready, wb_ready = sem("wa_ready"), sem("wb_ready")
        bias_ready = sem("bias_ready")
        slope_ready = sem("slope_ready")
        fin_step, fin_done = sem("fin_step"), sem("fin_done")
        scored = sem("scored")
        rs_ready = sem("rs_ready")
        prob_ready = sem("prob_ready")
        tr_free = sem("tr_free")
        ot_free = sem("ot_free")
        v_ready = sem("v_ready")
        stat_ready = sem("stat_ready")
        var_ready = sem("var_ready")
        newton = sem("newton")
        rows_ready = sem("rows_ready")
        po_free = sem("po_free")
        gate_step, gate_ready = sem("gate_step"), sem("gate_ready")
        small_ready = sem("small_ready")
        lora_ready = sem("lora_ready")
        lora_scaled = sem("lora_scaled")
        weff_ready = sem("weff_ready")
        ln_stat, ln_newton, ln_ready = sem("ln_stat"), sem("ln_newton"), sem("ln_ready")
        ln_var = sem("ln_var")
        ln_log, ln_r0 = sem("ln_log"), sem("ln_r0")

        passed = sem("passed")

        CONSTS = 8 + 7

        def wait_alone(eng, semaphore, value):
            eng.wait_ge(semaphore, value)
            eng.nop().then_inc(passed, 1)

        block = ctx.enter_context(nc.Block())

        @block.sync
        def _(sp):
            sp.nop().then_inc(gate_out[0], 16)
            sp.nop().then_inc(gate_out[1], 16)
            sp.nop().then_inc(res_out[0], 16)
            sp.nop().then_inc(res_out[1], 16)
            sp.dma_start(xtok[:], x_last).then_inc(x_in, 16)
            for dst, src in ((ident_sb, ident), (rel_sb, rel), (slope0, slopes), (qw_sb, qw),
                             (kw_sb, kw), (fb, ffn_b), (slope, slopes)):
                sp.dma_start(dst[:], src).then_inc(const_in, 16)
            for n in range(8):
                sp.dma_start(lw_sb[16 * n:16 * n + 16, :],
                             lw[n:n + 1, :].to_broadcast([16, 1])).then_inc(const_in, 16)
            sp.dma_start(stage_b[:, 0, :], lora_a).then_inc(lora_in, 16)
            sp.dma_start(stage_b[:, 1, :], lora_bt).then_inc(lora_in, 16)

            def load_a(pos, tile, dram):
                for half in range(2):
                    sp.wait_ge(wa_ready, pos.at(6, 2 * tile + half + 1))
                    sp.dma_start(stage_a[:, half, :], wa[dram * 2 + half]).then_inc(a_in[half], 16)

            def load_b(src, slot, free):
                sp.wait_ge(wb_ready, free)
                sp.dma_start(stage_b[:, slot, :], src).then_inc(b_in[slot], 16)

            def store_gate(b8, c):
                sp.wait_ge(gate_ready, b8 + (c + 1))
                sp.dma_start(gate_dram[c], x_buf[:, c % 2, :]).then_inc(gate_out[c % 2], 16)

            for half in range(2):
                sp.dma_start(stage_a[:, half, :], wa[half]).then_inc(a_in[half], 16)
            for k in range(NK):
                if k >= 4:
                    sp.wait_ge(weff_out[k - 4], 16)
                sp.dma_start(acc[:, 2 * (k % 4):2 * (k % 4) + 2, :].rearrange("p a n -> p (a n)"),
                             wT[k]).then_inc(wt_in[k % 4], 16)
                if k == 3:
                    for half in range(2):
                        sp.wait_ge(wa_ready, SLOT2 + half + 1)
                        sp.dma_start(stage_a[:, half, :], wa[2 + half]).then_inc(a_in[half], 16)
                if k >= 3:
                    for m in ([0] if k == 3 else [k - 3]):
                        sp.wait_ge(weff_ready, 2 * m + 2)
                        sp.dma_start(weff.rearrange("c d (k o) -> d c k o", k=NK)[:, :, m, :],
                                     acc[:, 2 * (m % 4):2 * (m % 4) + 2, :].rearrange(
                                         "p a (c o) -> p (a c) o", o=P)).then_inc(weff_out[m % 4], 16)
            for m in range(NK - 3, NK):
                sp.wait_ge(weff_ready, 2 * m + 2)
                sp.dma_start(weff.rearrange("c d (k o) -> d c k o", k=NK)[:, :, m, :],
                             acc[:, 2 * (m % 4):2 * (m % 4) + 2, :].rearrange(
                                 "p a (c o) -> p (a c) o", o=P)).then_inc(weff_out[m % 4], 16)
            sp.wait_ge(lora_ready, 4)
            for i in range(4):
                sp.wait_ge(weff_out[i], 32)

            with sp.Fori(0, BATCH) as b:
                pos = Pos(sp, b, 0)
                b8, b40 = sp.snap(b * 8), sp.snap(b * 40)
                sp.wait_ge(tr_done, pos.tb(-2))
                sp.wait_ge(ln_ready, b * 4 + 4)
                sp.dma_start(xtok[:], x_tok[bass.ds(b, 1)].rearrange("o p t d -> (o p) t d")
                             ).then_inc(x_in, 16)
                load_b(weff[0], 0, b40 + 1)
                load_b(weff[1], 1, b40 + 2)
                load_b(weff[2], 0, b40 + 3)
                load_a(pos, Q23, Q23)
                load_b(weff[3], 1, b40 + 4)
                store_gate(b8, 0)
                store_gate(b8, 1)
                load_b(weff[4], 0, b40 + 5)
                load_a(pos, 3, 3)
                load_b(weff[5], 1, b40 + 6)
                store_gate(b8, 2)
                store_gate(b8, 3)
                load_b(weff[6], 0, b40 + 7)
                load_a(pos, 4, 4)
                load_b(wo[0], 1, b40 + 8)
                store_gate(b8, 4)
                store_gate(b8, 5)
                load_b(weff[7], 0, b40 + 9)
                load_b(wo[1], 1, b40 + 10)
                store_gate(b8, 6)
                load_b(wo[2], 0, b40 + 11)
                load_a(pos, 5, 5)
                store_gate(b8, 7)

                def body(pos, g, last):
                    f = sp.snap(b * 40 + g * 4)
                    load_b(wo[g * 4 - 1], 1, f + 8)
                    load_a(pos, 3, 0 if last else g * 3 + 3)
                    load_b(wo[g * 4], 0, f + 9)
                    load_a(pos, 4, 1 if last else g * 3 + 4)
                    load_b(wo[g * 4 + 1], 1, f + 10)
                    load_b(wo[g * 4 + 2], 0, f + 11)
                    if not last:
                        load_a(pos, 5, g * 3 + 5)

                with sp.Fori(0, 3) as pair:
                    for h in range(2):
                        g = sp.snap(pair * 2 + (1 + h))
                        body(Pos(sp, b, g), g, False)
                body(Pos(sp, b, 7), 7, True)
                load_b(wo[31], 1, b40 + 40)
                for i in range(2):
                    sp.wait_ge(gate_out[i], b * 64 + 64 + 16)
                for c in range(NK + 2):
                    if c >= 2:
                        sp.wait_ge(fin_done, b8 + c)
                        sp.dma_start(outT[bass.ds(b * 8 + (c - 2), 1)].rearrange("o p n -> (o p) n"),
                                     x_buf[:, c % 2, :]).then_inc(res_out[c % 2], 16)
                    if c < NK:
                        if c >= 2:
                            sp.wait_ge(res_out[c % 2], b * 64 + 16 * (c // 2) + 16)
                        sp.dma_start(g_buf[:, c % 2, :], gate_dram[c]).then_inc(fin_in[c % 2], 16)
                        sp.dma_start(x_buf[:, c % 2, :],
                                     xT[bass.ds(b * 8 + c, 1)].rearrange("o p n -> (o p) n")
                                     ).then_inc(fin_in[c % 2], 16)
            for i in range(2):
                sp.wait_ge(res_out[i], 64 * BATCH + 16)
                sp.wait_ge(gate_out[i], 64 * BATCH + 16)
            sp.wait_ge(x_in, 16 * (BATCH + 1))

        @block.tensor
        def _(pe):
            pe.nop().then_inc(po_done, PO_LEAD)
            pe.nop().then_inc(pv_done, 1)
            pe.nop().then_inc(tr_done, 1)
            before = [None, None]
            turn = [0]

            def proj_bank(release):
                n = turn[0] % 2
                if before[n] is not None:
                    pe.wait_ge(*before[n])
                before[n] = release
                turn[0] += 1
                return proj_ps[n]

            def three(out, hi_l, lo_l, hi_r, lo_r, first, last):
                pe.matmul(out, hi_l, hi_r, start=first, stop=False)
                pe.matmul(out, hi_l, lo_r, start=False, stop=False)
                return pe.matmul(out, lo_l, hi_r, start=False, stop=last)

            def project(pos, tile, t):
                slot = tile_slot(pos, tile)
                bank = proj_bank((a_free, pos.at(12, 4 * tile + t + 1 + 1)))
                if t == 0:
                    pe.wait_ge(wa_ready, pos.at(6, 2 * tile + 2 + SLOT2))
                for k in range(NK):
                    cols = slice(t * P, t * P + P)
                    w = slice(k * 256, k * 256 + 256)
                    mm = three(bank[:, 0:256], xn_hi[:, k, cols], xn_lo[:, k, cols],
                               wa_hi[:, slot, w], wa_lo[:, slot, w], k == 0, k == NK - 1)
                mm.then_inc(a_done, 1)

            def gate(index, c):
                slot = c % 2 if c < 7 else 0
                bank = proj_bank((po_free, index(1 + SLOT2)))
                pe.wait_ge(wb_ready, gate_pieces(c))
                for k in range(NK):
                    w = slice(k * P, k * P + P)
                    mm = three(bank[:], wb_hi[:, slot, w], wb_lo[:, slot, w],
                               xn_hi[:, k, :], xn_lo[:, k, :], k == 0, k == NK - 1)
                mm.then_inc(po_done, 1)

            def out_proj(pos, pair, j, at, chunks):
                slot = j % 2
                for c in chunks:
                    bank = proj_bank((po_free, pos.po(at + c + 1 + SLOT2)))
                    for hh in range(2):
                        w = slice(hh * 512 + c * P, hh * 512 + c * P + P)
                        mm = three(bank[:], wb_hi[:, slot, w], wb_lo[:, slot, w],
                                   o_hi[:, pair, hh, :], o_lo[:, pair, hh, :], hh == 0, hh == 1)
                    mm.then_inc(po_done, 1)

            def scores(pos, j):
                if j == 0:
                    pe.wait_ge(tr_free, pos.tb(0 + SLOT2))
                else:
                    pe.wait_ge(tr_free, pos.tb(5 * j + SLOT2))
                for i in range(NT):
                    pe.wait_ge(scored, pos.at(16, 4 * j + i + 1))
                    out = sc_ps[i % 2][:, 0:P * (i + 1)]
                    q = slice(i * P, i * P + P)
                    k = slice(0, P * (i + 1))
                    three(out, qT_hi[:, j % 2, q], qT_lo[:, j % 2, q], kT_hi[:, k], kT_lo[:, k],
                          True, True).then_inc(s_done, 1)

            def attend(pos, j):
                if j == 0:
                    pe.wait_ge(v_ready, pos.at(1, 1))
                pe.wait_ge(tr_free, pos.tb(5 * j + 4 + SLOT2))
                pe.wait_ge(ot_free, pos.at(4, j + 1))
                for k in range(NT):
                    w = slice(PT_AT[k], PT_AT[k] + S - P * k)
                    mm = three(ot_ps[:, P * k:S], v_hi[:, k, :], v_lo[:, k, :],
                               pT_hi[:, w], pT_lo[:, w], k == 0, k == NT - 1)
                mm.then_inc(pv_done, 1)

            def turn_bank(pos, c, parity):
                pe.wait_ge(tr_free, pos.tb(c + 1))
                return tr_ps[parity % 2]

            def turn_probs(pos, j, gp):
                pe.wait_ge(prob_ready, pos.at(4, j + 1))
                for k in range(NT):
                    bank = turn_bank(pos, 5 * j + k, gp + 5 * j + k)
                    for i in range(k, NT):
                        a = P_AT[i] + k * P
                        mm = pe.transpose(bank[:, i * P:i * P + P], prob[:, a:a + P], ident_sb[:])
                    mm.then_inc(tr_done, 1)

            def turn_rows(pos, rows, col, c, parity, tile):
                pe.wait_ge(rows_ready, pos.at(3, tile + 1))
                bank = turn_bank(pos, c, parity)
                for t in range(NT):
                    mm = pe.transpose(bank[:, t * P:t * P + P], rows[:, t, col:col + P], ident_sb[:])
                mm.then_inc(tr_done, 1)

            def turn_queries(pos, j, c, parity):
                tile = {1: Q01, 2: Q23, 3: Q23, 4: 3 + Q01, 0: Q01}[j]
                turn_rows(pos, raw[tile % 3], (j % 2) * HD, c, parity, tile)

            def turn_x(pos, c0):
                for c in range(NK):
                    bank = turn_bank(pos, c0 + c, c)
                    for t in range(NT):
                        mm = pe.transpose(bank[:, t * P:t * P + P], xtok[:, t, c * P:c * P + P],
                                          ident_sb[:])
                    mm.then_inc(tr_done, 1)

            pe.wait_ge(const_in, 16 * CONSTS)
            pe.wait_ge(ln_ready, 4)
            for c in range(NK):
                pe.wait_ge(tr_free, c + 1)
                for t in range(NT):
                    mm = pe.transpose(tr_ps[c % 2][:, t * P:t * P + P], xtok[:, t, c * P:c * P + P],
                                      ident_sb[:])
                mm.then_inc(tr_done, 1)
            pe.wait_ge(lora_ready, 4)
            for n in range(2 * NK):
                if n >= 2:
                    pe.wait_ge(weff_ready, n - 1)
                k, half = divmod(n, 2)
                a, o = slice(k * P, k * P + P), slice(half * 512, half * 512 + 512)
                three(proj_ps[n % 2][:], o_hi[:, 0].rearrange("p h s -> p (h s)")[:, a],
                      o_lo[:, 0].rearrange("p h s -> p (h s)")[:, a],
                      o_hi[:, 1].rearrange("p h s -> p (h s)")[:, o],
                      o_lo[:, 1].rearrange("p h s -> p (h s)")[:, o], True, True
                      ).then_inc(weff_done, 1)
            pe.wait_ge(weff_ready, 2 * NK)

            def tile_slot(pos, tile):
                return (pos.parity + tile) % 2

            def body(pos, gp, first, last):
                pos.parity = gp
                for j in range(G):
                    scores(pos, j)
                    if j > 0:
                        attend(pos, j - 1)
                    elif not first:
                        pe.wait_ge(tr_free, pos.tb(SLOT2 - 2))
                        pe.wait_ge(ot_free, pos.at(4, 0))
                        for k in range(NT):
                            w = slice(PT_AT[k], PT_AT[k] + S - P * k)
                            mm = three(ot_ps[:, P * k:S], v_hi[:, k, :], v_lo[:, k, :],
                                       pT_hi[:, w], pT_lo[:, w], k == 0, k == NT - 1)
                        mm.then_inc(pv_done, 1)
                    if first:
                        gate(lambda c, j=j: pos.po([2, 4, 6, 11][j] + c), [2, 4, 6, 7][j])
                    for tile, t in PROJ[j]:
                        tile += 0 if tile == Q23 else 3
                        if last and tile != Q23:
                            continue
                        project(pos, tile, t)
                    late_gate = first and j < 2
                    pair = 0 if j >= 2 else 1
                    at = [None, None, 7, 12][j] if first else 4 * j
                    if not late_gate:
                        pe.wait_ge(wb_ready, out_pieces(pos, j, first))
                        pe.wait_ge(ot_free, pos.at(4, 2 + 1 if j >= 2 else 0 + 1))
                        out_proj(pos, pair, 1 if first else j, at, (0, 1))
                    turn_probs(pos, j, gp)
                    if j < 3:
                        turn_queries(pos, j + 1, 5 * j + 4, gp + 5 * j + 4)
                    elif not last:
                        turn_rows(pos, raw[KV], 0, 19, gp + 19, 3 + KV)
                        turn_queries(pos, 4, 20, gp + 20)
                    if late_gate:
                        gate(lambda c, j=j: pos.po([3, 5][j] + c), [3, 5][j])
                    else:
                        out_proj(pos, pair, 1 if first else j, at, (2, 3))

            def out_pieces(pos, j, first):
                if first:
                    return pos.at(0, [0, 0, 8, 10][j] + SLOT2, 40)
                return pos.at(4, 7 + j + SLOT2, 8)

            with pe.Fori(0, BATCH) as b:
                turn[0] = 0
                pos = Pos(pe, b, 0)
                pos.parity = 0
                gate_pieces = lambda c: pos.at(0, [1, 2, 3, 4, 5, 6, 7, 9][c] + SLOT2, 40)
                before[0], before[1] = (po_free, pos.po(-1 + SLOT2)), (po_free, pos.po(0 + SLOT2))
                pe.wait_ge(tr_free, pos.tb(-2 + SLOT2))
                for tile in (KV, Q01):
                    for t in range(NT):
                        project(pos, tile, t)
                gate(lambda c: pos.po(0 + c), 0)
                turn_rows(pos, raw[KV], 0, -2, 0, KV)
                turn_queries(pos, 0, -1, 1)
                gate(lambda c: pos.po(1 + c), 1)
                body(pos, 0, True, False)
                with pe.Fori(0, 3) as pair:
                    for h in range(2):
                        g = pair * 2 + (1 + h)
                        p = Pos(pe, b, g)
                        before[0], before[1] = (po_free, p.po(-1 + SLOT2)), (po_free, p.po(SLOT2))
                        turn[0] = 0
                        body(p, (1 + h) % 2, False, False)
                p = Pos(pe, b, 7)
                before[0], before[1] = (po_free, p.po(-1 + SLOT2)), (po_free, p.po(SLOT2))
                turn[0] = 0
                body(p, 1, False, True)
                attend(p, 3)
                pe.wait_ge(ln_ready, b * 4 + 8)
                turn_x(p, 19)
                for j in range(2):
                    pe.wait_ge(wb_ready, p.at(4, 11 + j + SLOT2, 8))
                    if j == 0:
                        pe.wait_ge(ot_free, p.at(4, 4 + 1))
                    out_proj(p, 1, j, 16 + 4 * j, range(4))

        @block.scalar
        def _(act):
            act.nop().then_inc(a_free, 1)
            act.wait_ge(const_in, 16 * CONSTS)
            act.preload_act_table_set("natural_log_exp_and_others")

            def split_a(pos, tile, parity, used):
                slot = (parity + tile) % 2
                for half in range(2):
                    act.wait_ge(a_in[half], pos.at(48, 16 * (tile + 1)))
                    if half == 0 and used is not None:
                        act.wait_ge(*used)
                    act.activation(wa_hi[:, slot, half * TILE:(half + 1) * TILE], stage_a[:, half, :],
                                   ACT.Copy).then_inc(wa_hi_done, 1)

            def split_b(slot, landed, used):
                act.wait_ge(b_in[slot], landed)
                act.wait_ge(po_done, used)
                act.activation(wb_hi[:, slot, :], stage_b[:, slot, :], ACT.Copy).then_inc(wb_hi_done, 1)

            def copy_rows(pos, tile, t):
                act.wait_ge(a_done, pos.at(12, 4 * tile + t + 1))
                act.activation(raw[tile % 3][:, t, :], proj_ps[turn[0] % 2][:, 0:256], ACT.Copy
                               ).then_inc(a_free, 1)

            def rsqrt(pos, tile, n):
                act.wait_ge(var_ready, pos.at(3, tile + 1))
                act.activation(lnv[:, 0:n], var[:, 0:n], ACT.Ln).then_inc(ln_done, 1)
                act.wait_ge(ln_done, pos.at(3, tile + 1))
                act.activation(rinv[:, 0:n], lnv[:, 0:n], ACT.Exp, scale=-0.5).then_inc(r0_done, 1)

            def take_hi(pos, c, parity, dst, src=None, scale=1.0):
                act.wait_ge(tr_done, pos.tb(c + 1 + 1))
                bank = tr_ps[parity % 2][:]
                act.activation(dst, bank if src is None else bank[:, src], ACT.Copy, scale=scale
                               ).then_inc(tr_hi, 1)

            def exps(pos, j):
                for i in range(NT):
                    act.wait_ge(scored, pos.at(16, 4 * j + i + 1 + SLOT2))
                    p = prob[:, P_AT[i]:P_AT[i] + P * (i + 1)]
                    act.activation(p, p, ACT.Exp, bias=negmax[:, i:i + 1], scale=-1.0,
                                   accum_out=rowsum[:, i:i + 1]).then_inc(exp_done, 1)

            def head_out(pos, j, pair, hh):
                act.wait_ge(pv_done, pos.at(4, j + 1 + 1))
                act.activation(o_hi[:, pair, hh, :], ot_ps[:], ACT.Copy).then_inc(ot_hi, 1)

            def gate_exp_of(pos, c, at, bank):
                act.wait_ge(po_done, pos.po(at + 1 + PO_LEAD))
                if c < 2:
                    act.wait_ge(fin_done, pos.at(0, 1, 8))
                else:
                    act.wait_ge(gate_ready, pos.at(0, c - 1, 8))
                act.activation(g_buf[:, c % 2, :], proj_ps[bank][:], ACT.Exp, scale=-1.0,
                               bias=nfb[:, c:c + 1]).then_inc(gate_exp, 1)

            turn = [0]

            act.wait_ge(ln_var, 1)
            act.activation(lnv[:, 0:NT], var[:, 0:NT], ACT.Ln).then_inc(ln_log, 1)
            act.wait_ge(ln_log, 1)
            act.activation(rinv[:, 0:NT], lnv[:, 0:NT], ACT.Exp, scale=-0.5).then_inc(ln_r0, 1)
            act.wait_ge(lora_in, 32)
            act.activation(o_hi[:, 0].rearrange("p h s -> p (h s)"), stage_b[:, 0, :], ACT.Copy
                           ).then_inc(lora_hi, 1)
            act.wait_ge(lora_scaled, 1)
            act.activation(o_hi[:, 1].rearrange("p h s -> p (h s)"), stage_b[:, 1, :], ACT.Copy
                           ).then_inc(lora_hi, 1)
            for tile in (KV, Q01):
                for half in range(2):
                    act.wait_ge(a_in[half], 16 * (tile + 1))
                    act.activation(wa_hi[:, tile, half * TILE:(half + 1) * TILE],
                                   stage_a[:, half, :], ACT.Copy).then_inc(wa_hi_done, 1)
            for c in range(NK):
                act.wait_ge(tr_done, c + 1 + 1)
                act.activation(xn_hi[:, c, :], tr_ps[c % 2][:], ACT.Copy).then_inc(tr_hi, 1)

            def body(pos, gp, first, last):
                for j in range(G):
                    exps(pos, j)
                    if not (first and j == 0):
                        head_out(pos, j - 1, 0 if j in (1, 2) else 1, (j - 1) % 2)
                    if j == 0:
                        act.activation(v_hi[:], raw[KV][:, :, HD:2 * HD], ACT.Copy
                                       ).then_inc(v_hi_done, 1)
                    if first:
                        split_b(1, pos.at(0, 16 * (2 + j), 320), pos.po([2, 4, 6, 11][j] + PO_LEAD))
                        bank = turn[0] % 2
                        turn[0] += 1
                        c, at = [(2, 2), (4, 4), (6, 6), (7, 11)][j]
                        gate_exp_of(pos, c, at, bank)
                        split_b(0, pos.at(0, 16 * (3 + j), 320), pos.po([3, 5, 7, 12][j] + PO_LEAD))
                    else:
                        split_b((j + 1) % 2, pos.at(32, 16 * (4 + (j + 1) // 2), 64),
                                pos.po(4 * j + PO_LEAD))
                    if j == 0:
                        split_a(pos, 3 + KV, gp, (a_done, pos.at(12, 8)))
                    for tile, t in PROJ[j]:
                        tile += 0 if tile == Q23 else 3
                        if last and tile != Q23:
                            continue
                        if t == 0 and tile % 3 == KV:
                            act.wait_ge(v_ready, pos.at(1, 1))
                        copy_rows(pos, tile, t)
                        turn[0] += 1
                        if t == 3:
                            rsqrt(pos, tile, 4 if tile % 3 == KV else 8)
                    if j == 1:
                        split_a(pos, 3 + Q01, gp, (a_done, pos.at(12, 12)))
                    if j == 3 and not last:
                        split_a(pos, 3 + Q23, gp, (a_done, pos.at(12, 16)))
                    if not (first and j < 2):
                        turn[0] += 2
                    for k in range(NT):
                        w = slice(PT_AT[k], PT_AT[k] + S - P * k)
                        take_hi(pos, 5 * j + k, gp + 5 * j + k, pT_hi[:, w], slice(P * k, S))
                    if j < 3:
                        take_hi(pos, 5 * j + 4, gp + 5 * j + 4, qT_hi[:, (j + 1) % 2, :])
                    elif not last:
                        take_hi(pos, 19, gp + 19, kT_hi[:], scale=qkw[:, 0:1])
                        take_hi(pos, 20, gp + 20, qT_hi[:, 0, :])
                    if first and j < 2:
                        bank = turn[0] % 2
                        turn[0] += 1
                        gate_exp_of(pos, [3, 5][j], [3, 5][j], bank)
                    else:
                        turn[0] += 2

            act.wait_ge(small_ready, 2)
            with act.Fori(0, BATCH) as b:
                turn[0] = 0
                pos = Pos(act, b, 0)
                split_b(0, pos.at(0, 16, 320), pos.po(-4 + PO_LEAD))
                for t in range(NT):
                    copy_rows(pos, KV, t)
                    turn[0] += 1
                rsqrt(pos, KV, 4)
                split_b(1, pos.at(0, 16, 320), pos.po(0 + PO_LEAD))
                split_a(pos, Q23, 0, (a_done, pos.at(12, 4)))
                for t in range(NT):
                    copy_rows(pos, Q01, t)
                    turn[0] += 1
                rsqrt(pos, Q01, 8)
                gate_exp_of(pos, 0, 0, 0)
                split_b(0, pos.at(0, 32, 320), pos.po(1 + PO_LEAD))
                take_hi(pos, -2, 0, kT_hi[:], scale=qkw[:, 0:1])
                take_hi(pos, -1, 1, qT_hi[:, 0, :])
                gate_exp_of(pos, 1, 1, 1)
                turn[0] = 0
                body(pos, 0, True, False)
                with act.Fori(0, 3) as pair:
                    for h in range(2):
                        turn[0] = 0
                        body(Pos(act, b, pair * 2 + (1 + h)), (1 + h) % 2, False, False)
                turn[0] = 0
                p = Pos(act, b, 7)
                body(p, 1, False, True)
                head_out(p, 3, 1, 1)
                split_b(1, p.at(32, 96, 64), p.po(16 + PO_LEAD))
                act.wait_ge(ln_var, b + 2)
                act.activation(lnv[:, 0:NT], var[:, 0:NT], ACT.Ln).then_inc(ln_log, 1)
                act.wait_ge(ln_log, b + 2)
                act.activation(rinv[:, 0:NT], lnv[:, 0:NT], ACT.Exp, scale=-0.5).then_inc(ln_r0, 1)
                for c in range(NK):
                    take_hi(p, 19 + c, c, xn_hi[:, c, :])

        @block.gpsimd
        def _(pool):
            pool.nop().then_inc(wa_ready, SLOT2)
            pool.nop().then_inc(wb_ready, SLOT2)
            pool.nop().then_inc(fin_done, 1)
            pool.wait_ge(const_in, 16 * CONSTS)

            def low_a(pos, tile, parity):
                slot = (parity + tile) % 2
                for half in range(2):
                    w = slice(half * TILE, (half + 1) * TILE)
                    pool.wait_ge(wa_hi_done, pos.at(6, 2 * tile + half + 1))
                    pool.tensor_tensor(wa_lo[:, slot, w], stage_a[:, half, :], wa_hi[:, slot, w],
                                       ALU.subtract).then_inc(wa_ready, 1)

            def low_b(slot, made):
                pool.wait_ge(wb_hi_done, made)
                pool.tensor_tensor(wb_lo[:, slot, :], stage_b[:, slot, :], wb_hi[:, slot, :],
                                   ALU.subtract).then_inc(wb_ready, 1)

            def bias_of(pos, j):
                wait_alone(pool, scored, pos.at(16, 4 * j - 4 + SLOT2))
                pool.tensor_scalar(bias_sb[:, j % 2, :], rel_sb[:], slope[:, j % 4:j % 4 + 1], None,
                                   ALU.mult).then_inc(bias_ready, 1)

            pool.tensor_scalar(bias_sb[:, 0, :], rel_sb[:], slope[:, 0:1], None, ALU.mult
                               ).then_inc(bias_ready, 1)
            for tile in (KV, Q01):
                for half in range(2):
                    w = slice(half * TILE, (half + 1) * TILE)
                    pool.wait_ge(wa_hi_done, 2 * tile + half + 1)
                    pool.tensor_tensor(wa_lo[:, tile, w], stage_a[:, half, :], wa_hi[:, tile, w],
                                       ALU.subtract).then_inc(wa_ready, 1)

            def body(pos, gp, first, last):
                for j in range(G):
                    if j == 3:
                        wait_alone(pool, bias_ready, pos.at(4, 4))
                        if last:
                            pool.tensor_copy(slope[:], slope0[:]).then_inc(slope_ready, 1)
                        else:
                            pool.tensor_scalar(slope[:], slope[:], 0.5, None, ALU.mult
                                               ).then_inc(slope_ready, 1)
                        wait_alone(pool, slope_ready, pos.at(1, 1))
                    if not first:
                        low_b((j + 1) % 2, pos.at(4, 8 + j, 8))
                    else:
                        low_b(1, pos.at(0, 4 + 2 * j, 40))
                    bias_of(pos, j + 1)
                    if first:
                        low_b(0, pos.at(0, 5 + 2 * j, 40))
                    if j == 0:
                        low_a(pos, 3 + KV, gp)
                    if j == 1:
                        low_a(pos, 3 + Q01, gp)
                    if j == 3 and not last:
                        low_a(pos, 3 + Q23, gp)

            with pool.Fori(0, BATCH) as b:
                pos = Pos(pool, b, 0)
                low_b(0, pos.at(0, 1, 40))
                low_b(1, pos.at(0, 2, 40))
                low_a(pos, Q23, 0)
                low_b(0, pos.at(0, 3, 40))
                body(pos, 0, True, False)
                with pool.Fori(0, 3) as pair:
                    for h in range(2):
                        body(Pos(pool, b, pair * 2 + (1 + h)), (1 + h) % 2, False, False)
                p = Pos(pool, b, 7)
                body(p, 1, False, True)
                low_b(1, p.at(4, 12, 8))
                for c in range(NK):
                    pool.wait_ge(fin_in[c % 2], b * 128 + 32 * (c // 2 + 1))
                    pool.wait_ge(po_free, p.po(16 + c + 1 + SLOT2))
                    pool.tensor_tensor(g_buf[:, c % 2, :], g_buf[:, c % 2, :], acc[:, c, :],
                                       ALU.mult).then_inc(fin_step, 1)
                    pool.wait_ge(fin_step, b * 8 + (c + 1))
                    pool.tensor_tensor(x_buf[:, c % 2, :], x_buf[:, c % 2, :], g_buf[:, c % 2, :],
                                       ALU.add).then_inc(fin_done, 1)

        @block.vector
        def _(dve):
            dve.nop().then_inc(scored, SLOT2)
            dve.nop().then_inc(tr_free, SLOT2)
            dve.nop().then_inc(po_free, SLOT2)
            dve.nop().then_inc(ot_free, 1)
            dve.wait_ge(const_in, 16 * CONSTS)
            dve.tensor_tensor(qkw[:], qw_sb[:], kw_sb[:], ALU.mult).then_inc(small_ready, 1)
            dve.tensor_scalar(nfb[:], fb[:], -1.0, None, ALU.mult).then_inc(small_ready, 1)

            def newton_step(n, count, done, base):
                dve.tensor_tensor(tmp[:, 0:n], rinv[:, 0:n], rinv[:, 0:n], ALU.mult).then_inc(done, 1)
                dve.wait_ge(done, count(1))
                dve.tensor_tensor(tmp[:, 0:n], tmp[:, 0:n], var[:, 0:n], ALU.mult).then_inc(done, 1)
                dve.wait_ge(done, count(2))
                dve.tensor_scalar(tmp[:, 0:n], tmp[:, 0:n], -0.5, 1.5, ALU.mult, ALU.add
                                  ).then_inc(done, 1)
                dve.wait_ge(done, count(3))
                dve.tensor_tensor(rinv[:, 0:n], rinv[:, 0:n], tmp[:, 0:n], ALU.mult).then_inc(done, 1)
                dve.wait_ge(done, count(4))

            def layer_norm(loaded, r):
                dve.wait_ge(x_in, loaded)
                for t in range(NT):
                    for i in range(2):
                        ins = dve.bn_stats(bn[:, t, 6 * i:6 * i + 6], xtok[:, t, 512 * i:512 * i + 512])
                ins.then_inc(ln_stat, 1)
                wait_alone(dve, ln_stat, r(2, 1))
                for t in range(NT):
                    ins = dve.bn_aggr(mv[:, t, :], bn[:, t, :])
                ins.then_inc(ln_stat, 1)
                dve.wait_ge(ln_stat, r(2, 2))
                dve.tensor_scalar(var[:, 0:NT], mv[:, :, 1], LN_EPS, None, ALU.add).then_inc(ln_var, 1)
                dve.wait_ge(ln_r0, r(1, 1))
                newton_step(NT, lambda c: r(4, c), ln_newton, None)
                for t in range(NT):
                    dve.tensor_scalar(xtok[:, t, :], xtok[:, t, :], mv[:, t, 0:1], rinv[:, t:t + 1],
                                      ALU.subtract, ALU.mult).then_inc(ln_ready, 1)

            def row_stats(pos, tile, t):
                heads = 1 if tile % 3 == KV else 2
                dve.wait_ge(a_free, pos.at(12, 4 * tile + t + 1 + 1))
                for h in range(heads):
                    r = raw[tile % 3][:, t, h * HD:h * HD + HD]
                    at = t * heads + h
                    ins = dve.tensor_tensor_reduce(sq[:, at, :], r, r, 1.0, 0.0, ALU.mult, ALU.add,
                                                   ss[:, at:at + 1])
                if t == 3:
                    ins.then_inc(stat_ready, 1)

            def row_var(pos, tile):
                dve.wait_ge(stat_ready, pos.at(3, tile + 1))
                if tile % 3 == KV:
                    dve.tensor_scalar(var[:, 0:4], ss[:, 0:4], 1.0 / HD, RMS_EPS, ALU.mult, ALU.add
                                      ).then_inc(var_ready, 1)
                else:
                    dve.tensor_scalar(var[:], ss[:], HD * RMS_EPS, None, ALU.add
                                      ).then_inc(var_ready, 1)

            def scale_rows(pos, tile):
                n = 4 if tile % 3 == KV else 8
                dve.wait_ge(r0_done, pos.at(3, tile + 1))
                newton_step(n, lambda c: pos.at(12, 4 * tile + c), newton, None)
                if tile % 3 == KV:
                    r = raw[KV][:, :, 0:HD]
                    f = rinv[:, 0:4].unsqueeze(2).to_broadcast([P, NT, HD])
                else:
                    r = raw[tile % 3][:].rearrange("p t (h d) -> p (t h) d", h=2)
                    f = rinv[:].unsqueeze(2).to_broadcast([P, 8, HD])
                dve.tensor_tensor(r, r, f, ALU.mult).then_inc(rows_ready, 1)

            def take_lo(pos, c, parity, dst, hi, src=None, scale=None):
                dve.wait_ge(tr_hi, pos.tb(c + 1))
                bank = tr_ps[parity % 2][:]
                bank = bank if src is None else bank[:, src]
                if scale is None:
                    dve.tensor_tensor(dst, bank, hi, ALU.subtract).then_inc(tr_free, 1)
                else:
                    dve.scalar_tensor_tensor(out=dst, in0=bank, scalar=scale, in1=hi, op0=ALU.mult,
                                             op1=ALU.subtract).then_inc(tr_free, 1)

            def bias_and_max(pos, j):
                dve.wait_ge(bias_ready, pos.at(4, j + 1))
                for i in range(NT):
                    w = P * (i + 1)
                    wait_alone(dve, s_done, pos.at(16, 4 * j + i + 1))
                    dve.tensor_tensor_reduce(prob[:, P_AT[i]:P_AT[i] + w], sc_ps[i % 2][:, 0:w],
                                             bias_sb[:, j % 2, S - w:S], -1.0, 3e38,
                                             ALU.add, ALU.min, negmax[:, i:i + 1]).then_inc(scored, 1)

            def normalise(pos, j):
                dve.wait_ge(exp_done, pos.at(16, 4 * j + 4))
                dve.reciprocal(rs_inv[:], rowsum[:]).then_inc(rs_ready, 1)
                dve.wait_ge(rs_ready, pos.at(4, j + 1))
                for i in range(NT):
                    p = prob[:, P_AT[i]:P_AT[i] + P * (i + 1)]
                    ins = dve.tensor_scalar(p, p, rs_inv[:, i:i + 1], None, ALU.mult)
                ins.then_inc(prob_ready, 1)

            def head_out(pos, j, pair, hh):
                dve.wait_ge(ot_hi, pos.at(4, j + 1))
                dve.tensor_tensor(o_lo[:, pair, hh, :], ot_ps[:], o_hi[:, pair, hh, :], ALU.subtract
                                  ).then_inc(ot_free, 1)

            def add_out(pos, at, chunk, bank, copy):
                dve.wait_ge(po_done, pos.po(at + 1 + PO_LEAD))
                if copy:
                    dve.tensor_copy(acc[:, chunk, :], proj_ps[bank % 2][:]).then_inc(po_free, 1)
                else:
                    dve.tensor_tensor(acc[:, chunk, :], acc[:, chunk, :], proj_ps[bank % 2][:],
                                      ALU.add).then_inc(po_free, 1)

            def gate(pos, c, bank):
                e = g_buf[:, c % 2, :]
                dve.wait_ge(gate_exp, pos.at(0, c + 1, 8))
                dve.tensor_scalar(e, e, 1.0, None, ALU.add).then_inc(gate_step, 1)
                dve.wait_ge(gate_step, pos.at(0, 2 * c + 1, 16))
                dve.reciprocal(e, e).then_inc(gate_step, 1)
                dve.wait_ge(gate_step, pos.at(0, 2 * c + 2, 16))
                if c < 2:
                    dve.wait_ge(res_out[c], pos.at(0, 16, 64))
                dve.wait_ge(gate_out[c % 2], pos.at(0, 16 * (c // 2) + 16, 64))
                dve.scalar_tensor_tensor(out=x_buf[:, c % 2, :], in0=proj_ps[bank % 2][:],
                                         scalar=fb[:, c:c + 1], in1=e, op0=ALU.add, op1=ALU.mult
                                         ).then_inc(gate_ready, 1)
                dve.wait_ge(gate_ready, pos.at(0, c + 1, 8))
                dve.nop().then_inc(po_free, 1)

            layer_norm(16, lambda k, c: c)
            dve.wait_ge(lora_in, 32)
            dve.tensor_scalar(stage_b[:, 1, :], stage_b[:, 1, :], lw_sb[:, 0:1], LORA_SCALE,
                              ALU.mult, ALU.mult).then_inc(lora_scaled, 1)
            for i in range(2):
                dve.wait_ge(lora_hi, i + 1)
                dve.tensor_tensor(o_lo[:, i].rearrange("p h s -> p (h s)"), stage_b[:, i, :],
                                  o_hi[:, i].rearrange("p h s -> p (h s)"), ALU.subtract
                                  ).then_inc(lora_ready, 2)
            for c in range(NK):
                dve.wait_ge(tr_hi, c + 1)
                dve.tensor_tensor(xn_lo[:, c, :], tr_ps[c % 2][:], xn_hi[:, c, :], ALU.subtract
                                  ).then_inc(tr_free, 1)
            for n in range(2 * NK):
                k, half = divmod(n, 2)
                dve.wait_ge(wt_in[k % 4], 16 * (k // 4 + 1))
                dve.wait_ge(weff_done, n + 1)
                w = acc[:, 2 * (k % 4) + half, :]
                dve.tensor_tensor(w, w, proj_ps[n % 2][:], ALU.add).then_inc(weff_ready, 1)

            turn = [0]

            def body(pos, gp, first, last):
                for j in range(G):
                    bias_and_max(pos, j)
                    normalise(pos, j)
                    if not (first and j == 0):
                        head_out(pos, j - 1, 0 if j in (1, 2) else 1, (j - 1) % 2)
                    if j == 0:
                        dve.wait_ge(v_hi_done, pos.at(1, 1))
                        dve.tensor_tensor(v_lo[:], raw[KV][:, :, HD:2 * HD], v_hi[:], ALU.subtract
                                          ).then_inc(v_ready, 1)
                    if first:
                        gate(pos, [2, 4, 6, 7][j], turn[0])
                        turn[0] += 1
                    groups = []
                    for tile, t in PROJ[j]:
                        tile += 0 if tile == Q23 else 3
                        if last and tile != Q23:
                            continue
                        groups.append((tile, t))
                    ended = None
                    for tile, t in groups:
                        row_stats(pos, tile, t)
                        turn[0] += 1
                        if t == 3:
                            row_var(pos, tile)
                            if (tile, t) != groups[-1]:
                                scale_rows(pos, tile)
                            else:
                                ended = tile
                    adds = not (first and j < 2)
                    at = [None, None, 7, 12][j] if first else 4 * j
                    half = 4 * (j % 2)
                    if adds:
                        for c in range(2):
                            add_out(pos, at + c, half + c, turn[0], first)
                            turn[0] += 1
                    if ended is not None:
                        scale_rows(pos, ended)
                    for k in range(NT):
                        w = slice(PT_AT[k], PT_AT[k] + S - P * k)
                        take_lo(pos, 5 * j + k, gp + 5 * j + k, pT_lo[:, w], pT_hi[:, w],
                                slice(P * k, S))
                    if j < 3:
                        take_lo(pos, 5 * j + 4, gp + 5 * j + 4, qT_lo[:, (j + 1) % 2, :],
                                qT_hi[:, (j + 1) % 2, :])
                    elif not last:
                        take_lo(pos, 19, gp + 19, kT_lo[:], kT_hi[:], scale=qkw[:, 0:1])
                        take_lo(pos, 20, gp + 20, qT_lo[:, 0, :], qT_hi[:, 0, :])
                    if adds:
                        for c in range(2, 4):
                            add_out(pos, at + c, half + c, turn[0], first)
                            turn[0] += 1
                    else:
                        gate(pos, [3, 5][j], turn[0])
                        turn[0] += 1

            with dve.Fori(0, BATCH) as b:
                pos = Pos(dve, b, 0)
                for t in range(NT):
                    row_stats(pos, KV, t)
                row_var(pos, KV)
                scale_rows(pos, KV)
                for t in range(NT):
                    row_stats(pos, Q01, t)
                row_var(pos, Q01)
                scale_rows(pos, Q01)
                gate(pos, 0, 0)
                take_lo(pos, -2, 0, kT_lo[:], kT_hi[:], scale=qkw[:, 0:1])
                take_lo(pos, -1, 1, qT_lo[:, 0, :], qT_hi[:, 0, :])
                gate(pos, 1, 1)
                turn[0] = 0
                body(pos, 0, True, False)
                with dve.Fori(0, 3) as pair:
                    for h in range(2):
                        turn[0] = 0
                        body(Pos(dve, b, pair * 2 + (1 + h)), (1 + h) % 2, False, False)
                turn[0] = 0
                p = Pos(dve, b, 7)
                body(p, 1, False, True)
                head_out(p, 3, 1, 1)
                layer_norm(b * 16 + 32, lambda k, c: b * k + (k + c))
                for c in range(NK):
                    take_lo(p, 19 + c, c, xn_lo[:, c, :], xn_hi[:, c, :])
                for c in range(NK):
                    add_out(p, 16 + c, c, c, False)


def kernel(**inputs):
    import numpy as np
    import concourse.bacc as bacc
    from concourse.bass_utils import run_bass_kernel_spmd

    def f(name):
        return np.asarray(inputs[name])

    x = f("L0_attn_x")
    x_tok = x.reshape(BATCH, NT, P, D).transpose(0, 2, 1, 3)
    wq = f("L0_attn_Wq").T.reshape(2, 4, P, HKV, 2, 256)
    wk = f("L0_attn_Wk").T.reshape(2, 4, P, HKV, 1, HD)
    wv = f("L0_attn_Wv").T.reshape(2, 4, P, HKV, 1, HD)
    wkv = np.concatenate([wk, wv], axis=-1)
    wa = np.concatenate([wkv, wq], axis=4).transpose(3, 4, 0, 2, 1, 5).reshape(HKV * 6, P, TILE)
    wo = f("L0_attn_Wo").T.reshape(HKV, 2, 2, HD, 2, 512).transpose(0, 1, 4, 3, 2, 5)
    key = np.arange(S)[None, :] - np.arange(P)[:, None] - (S - P)
    start = 2.0 ** (-2.0 ** (-2.0))
    arrays = {
        "x_tok": np.roll(x_tok, -1, axis=0),
        "x_last": x_tok[0],
        "xT": x.transpose(0, 2, 1).reshape(BATCH * NK, P, S),
        "wa": wa,
        "wo": wo.reshape(HKV * 4, P, TILE),
        "wT": f("L0_ffn_W").T.reshape(NK, P, D),
        "lora_a": f("L0_ffn_lora_A").reshape(P, D),
        "lora_bt": f("L0_ffn_lora_B").transpose(0, 2, 1).reshape(P, D),
        "lw": f("L0_ffn_lora_weights").reshape(8, 1),
        "ffn_b": f("L0_ffn_bias").reshape(NK, P).T,
        "qw": f("L0_attn_q_norm_w").reshape(P, 1),
        "kw": f("L0_attn_k_norm_w").reshape(P, 1),
        "rel": np.where(key > 0, MASKED, key).astype(np.float32),
        "slopes": np.tile(np.array([start * start ** i for i in range(G)], np.float32), (P, 1)),
        "ident": np.eye(P, dtype=np.float32),
    }
    arrays = {k: np.ascontiguousarray(v) for k, v in arrays.items()}
    nc = bacc.Bacc("TRN2", target_bir_lowering=False, num_devices=1)
    args = [nc.dram_tensor(k, v.shape, F32, kind="ExternalInput").ap() for k, v in arrays.items()]
    outT = nc.dram_tensor("outT", (BATCH * NK, P, S), F32, kind="ExternalOutput").ap()
    build_layer(nc, *args, outT)
    got = run_bass_kernel_spmd(nc, [arrays], core_ids=[0]).results[0]["outT"]
    return np.ascontiguousarray(got.reshape(BATCH, D, S).transpose(0, 2, 1))
```

```python
from contextlib import ExitStack

import concourse.bass as bass
from concourse import mybir

ALU = mybir.AluOpType
ACT = mybir.ActivationFunctionType
F32 = mybir.dt.float32
F32R = mybir.dt.float32r

P = 128
BATCH, S, D = 4, 512, 1024
H, HKV, HD = 32, 8, 128
G = H // HKV
NT = S // P
NK = D // P
TILE = 1024
PW = P * NT * (NT + 1) // 2
RMS_EPS, LN_EPS = 1e-6, 1e-5
LORA_SCALE = 2.0
MASKED = -1e38

KV, Q01, Q23 = 0, 1, 2
PROJ = [[(Q23, t) for t in range(4)],
        [(KV, 0), (KV, 1), (KV, 2)],
        [(KV, 3), (Q01, 0), (Q01, 1)],
        [(Q01, 2), (Q01, 3)]]

P_AT = [P * i * (i + 1) // 2 for i in range(NT)]
PT_AT = [sum(S - P * m for m in range(k)) for k in range(NT)]

SLOT2 = 2
SLOT3 = 3
PO_LEAD = 8


class Pos:

    def __init__(self, eng, b, g):
        self.eng, self.b, self.kept = eng, b, {}
        self.n = b * HKV + g

    def at(self, k, c, kb=0):
        if (k, kb) not in self.kept:
            v = self.n * k + self.b * kb if kb else self.n * k
            self.kept[k, kb] = self.eng.snap(v)
        return self.kept[k, kb] + c

    def first(self, c):
        return self.at(16, c, 8)

    def po(self, c):
        return self.at(16, c - 2, 8)

    def tb(self, c):
        return self.at(21, c + 10, 8)


def build_layer(nc, x_tok, x_last, xT, wa, wo, wT, lora_a, lora_bt, lw, ffn_b, qw, kw, rel, slopes,
                ident, outT):
    with ExitStack() as ctx:
        def sb(name, shape, dt=F32):
            return ctx.enter_context(nc.sbuf_tensor(name, shape, dt))

        def ps(name):
            return ctx.enter_context(nc.psum_tensor(name, [P, 512], F32))

        def sem(name):
            return ctx.enter_context(nc.semaphore(name))

        weff = nc.dram_tensor("weff", [NK, P, TILE], F32).ap()
        gate_dram = nc.dram_tensor("gate_dram", [NK, P, S], F32).ap()

        xtok = sb("xtok", [P, NT, D])
        xn_hi, xn_lo = sb("xn_hi", [P, NK, S], F32R), sb("xn_lo", [P, NK, S], F32R)
        acc = sb("acc", [P, NK, S])
        stage_a, stage_b = sb("stage_a", [P, 2, TILE]), sb("stage_b", [P, 2, TILE])
        wa_hi, wa_lo = sb("wa_hi", [P, 2, 2 * TILE], F32R), sb("wa_lo", [P, 2, 2 * TILE], F32R)
        wb_hi, wb_lo = sb("wb_hi", [P, 2, TILE], F32R), sb("wb_lo", [P, 2, TILE], F32R)
        raw = [sb("kv_raw", [P, NT, 256]), sb("q01_raw", [P, NT, 256]), sb("q23_raw", [P, NT, 256])]
        qT_hi, qT_lo = sb("qT_hi", [P, 2, S], F32R), sb("qT_lo", [P, 2, S], F32R)
        kT_hi, kT_lo = sb("kT_hi", [P, S], F32R), sb("kT_lo", [P, S], F32R)
        v_hi, v_lo = sb("v_hi", [P, NT, HD], F32R), sb("v_lo", [P, NT, HD], F32R)
        prob = sb("prob", [P, PW])
        pT_hi, pT_lo = sb("pT_hi", [P, PW], F32R), sb("pT_lo", [P, PW], F32R)
        bias_sb = sb("bias_sb", [P, 2, S])
        o_hi, o_lo = sb("o_hi", [P, 2, 2, S], F32R), sb("o_lo", [P, 2, 2, S], F32R)
        g_buf, x_buf = sb("g_buf", [P, 2, S]), sb("x_buf", [P, 2, S])
        ident_sb, rel_sb = sb("ident_sb", [P, P]), sb("rel_sb", [P, S])
        slope0, slope = sb("slope0", [P, G]), sb("slope", [P, G])
        qw_sb, kw_sb, qkw = sb("qw_sb", [P, 1]), sb("kw_sb", [P, 1]), sb("qkw", [P, 1])
        fb, nfb, lw_sb = sb("fb", [P, NK]), sb("nfb", [P, NK]), sb("lw_sb", [P, 1])
        sq = sb("sq", [P, 8, HD])
        ss, var, rinv, tmp = (sb(n, [P, 8]) for n in ("ss", "var", "rinv", "tmp"))
        lnv = sb("lnv", [P, 8])
        var_x, rinv_x, tmp_x, lnv_x = (sb(n, [P, NT]) for n in ("var_x", "rinv_x", "tmp_x", "lnv_x"))
        negmax, rowsum, rs_inv = (sb(n, [P, NT]) for n in ("negmax", "rowsum", "rs_inv"))
        bn = sb("bn", [P, NT, 12])
        mv = sb("mv", [P, NT, 2])

        proj_ps = [ps("proj0"), ps("proj1")]
        sc_ps = [ps("sc0"), ps("sc1")]
        tr_ps = [ps("tr0"), ps("tr1"), ps("tr2")]
        ot_ps = ps("ot")

        const_in = sem("const_in")
        x_in = sem("x_in")
        a_in = [sem("a_in0"), sem("a_in1")]
        b_in = [sem("b_in0"), sem("b_in1")]
        lora_in = sem("lora_in")
        wt_in = [sem(f"wt_in{i}") for i in range(4)]
        weff_out = [sem(f"weff_out{i}") for i in range(4)]
        gate_out = [sem("gate_out0"), sem("gate_out1")]
        fin_in = [sem("fin_in0"), sem("fin_in1")]
        res_out = [sem("res_out0"), sem("res_out1")]
        a_done = sem("a_done")
        po_done = sem("po_done")
        s_done = sem("s_done")
        tr_done = sem("tr_done")
        pv_done = sem("pv_done")
        weff_done = sem("weff_done")
        a_free = sem("a_free")
        wa_hi_done, wb_hi_done = sem("wa_hi_done"), sem("wb_hi_done")
        exp_done = sem("exp_done")
        tr_hi = sem("tr_hi")
        ot_hi = sem("ot_hi")
        v_hi_done = sem("v_hi_done")
        ln_done, r0_done = sem("ln_done"), sem("r0_done")
        gate_exp = sem("gate_exp")
        lora_hi = sem("lora_hi")
        wa_ready, wb_ready = sem("wa_ready"), sem("wb_ready")
        bias_ready = sem("bias_ready")
        slope_ready = sem("slope_ready")
        fin_step, fin_done = sem("fin_step"), sem("fin_done")
        scored = sem("scored")
        rs_ready = sem("rs_ready")
        prob_ready = sem("prob_ready")
        tr_free = sem("tr_free")
        ot_free = sem("ot_free")
        v_ready = sem("v_ready")
        stat_ready = sem("stat_ready")
        var_ready = sem("var_ready")
        newton = sem("newton")
        rows_ready = sem("rows_ready")
        po_free = sem("po_free")
        gate_step, gate_ready = sem("gate_step"), sem("gate_ready")
        small_ready = sem("small_ready")
        lora_ready = sem("lora_ready")
        lora_scaled = sem("lora_scaled")
        weff_ready = sem("weff_ready")
        ln_stat, ln_newton, ln_ready = sem("ln_stat"), sem("ln_newton"), sem("ln_ready")
        ln_var = sem("ln_var")
        ln_log, ln_r0 = sem("ln_log"), sem("ln_r0")

        passed = sem("passed")

        CONSTS = 8 + 7

        def wait_alone(eng, semaphore, value):
            eng.wait_ge(semaphore, value)
            eng.nop().then_inc(passed, 1)

        block = ctx.enter_context(nc.Block())

        @block.sync
        def _(sp):
            sp.nop().then_inc(gate_out[0], 16)
            sp.nop().then_inc(gate_out[1], 16)
            sp.nop().then_inc(res_out[0], 16)
            sp.nop().then_inc(res_out[1], 16)
            sp.dma_start(xtok[:], x_last).then_inc(x_in, 16)
            for dst, src in ((ident_sb, ident), (rel_sb, rel), (slope0, slopes), (qw_sb, qw),
                             (kw_sb, kw), (fb, ffn_b), (slope, slopes)):
                sp.dma_start(dst[:], src).then_inc(const_in, 16)
            for n in range(8):
                sp.dma_start(lw_sb[16 * n:16 * n + 16, :],
                             lw[n:n + 1, :].to_broadcast([16, 1])).then_inc(const_in, 16)
            sp.dma_start(stage_b[:, 0, :], lora_a).then_inc(lora_in, 16)
            sp.dma_start(stage_b[:, 1, :], lora_bt).then_inc(lora_in, 16)

            def load_a(pos, tile, dram):
                for half in range(2):
                    sp.wait_ge(wa_ready, pos.at(6, 2 * tile + half + 1))
                    sp.dma_start(stage_a[:, half, :], wa[dram * 2 + half]).then_inc(a_in[half], 16)

            def load_b(src, slot, free):
                sp.wait_ge(wb_ready, free)
                sp.dma_start(stage_b[:, slot, :], src).then_inc(b_in[slot], 16)

            def store_gate(b8, c):
                sp.wait_ge(gate_ready, b8 + (c + 1))
                sp.dma_start(gate_dram[c], x_buf[:, c % 2, :]).then_inc(gate_out[c % 2], 16)

            for half in range(2):
                sp.dma_start(stage_a[:, half, :], wa[half]).then_inc(a_in[half], 16)
            for k in range(NK):
                if k >= 4:
                    sp.wait_ge(weff_out[k - 4], 16)
                sp.dma_start(acc[:, 2 * (k % 4):2 * (k % 4) + 2, :].rearrange("p a n -> p (a n)"),
                             wT[k]).then_inc(wt_in[k % 4], 16)
                if k == 3:
                    for half in range(2):
                        sp.wait_ge(wa_ready, SLOT2 + half + 1)
                        sp.dma_start(stage_a[:, half, :], wa[2 + half]).then_inc(a_in[half], 16)
                if k >= 3:
                    for m in ([0] if k == 3 else [k - 3]):
                        sp.wait_ge(weff_ready, 2 * m + 2)
                        sp.dma_start(weff.rearrange("c d (k o) -> d c k o", k=NK)[:, :, m, :],
                                     acc[:, 2 * (m % 4):2 * (m % 4) + 2, :].rearrange(
                                         "p a (c o) -> p (a c) o", o=P)).then_inc(weff_out[m % 4], 16)
            for m in range(NK - 3, NK):
                sp.wait_ge(weff_ready, 2 * m + 2)
                sp.dma_start(weff.rearrange("c d (k o) -> d c k o", k=NK)[:, :, m, :],
                             acc[:, 2 * (m % 4):2 * (m % 4) + 2, :].rearrange(
                                 "p a (c o) -> p (a c) o", o=P)).then_inc(weff_out[m % 4], 16)
            sp.wait_ge(lora_ready, 4)
            for i in range(4):
                sp.wait_ge(weff_out[i], 32)

            load_b(weff[0], 0, 1)
            load_b(weff[1], 1, 2)
            for half in range(2):
                sp.wait_ge(wa_ready, 4 + half - 2 + 1 + SLOT2)
                sp.dma_start(stage_a[:, half, :], wa[4 + half]).then_inc(a_in[half], 16)

            with sp.Fori(0, BATCH) as b:
                pos = Pos(sp, b, 0)
                b8, b40 = sp.snap(b * 8), sp.snap(b * 40)
                load_b(weff[2], 0, b40 + 3)
                sp.wait_ge(tr_done, pos.tb(-2))
                sp.dma_start(xtok[:], x_tok[bass.ds(b, 1)].rearrange("o p t d -> (o p) t d")
                             ).then_inc(x_in, 16)
                load_b(weff[3], 1, b40 + 4)
                store_gate(b8, 0)
                store_gate(b8, 1)
                load_b(weff[4], 0, b40 + 5)
                load_a(pos, 3, 3)
                load_b(weff[5], 1, b40 + 6)
                store_gate(b8, 2)
                load_b(wo[0], 0, b40 + 7)
                load_a(pos, 4, 4)
                store_gate(b8, 3)
                store_gate(b8, 4)
                load_b(wo[1], 1, b40 + 8)
                load_b(wo[2], 0, b40 + 9)
                store_gate(b8, 5)
                load_a(pos, 5, 5)

                with sp.Fori(0, 3) as pair:
                    for h in range(2):
                        g = sp.snap(pair * 2 + (1 + h))
                        p, f = Pos(sp, b, g), sp.snap(b * 40 + g * 4)
                        load_b(wo[g * 4 - 1], 1, f + 6)
                        load_a(p, 3, g * 3 + 3)
                        load_b(wo[g * 4], 0, f + 7)
                        load_a(p, 4, g * 3 + 4)
                        load_b(wo[g * 4 + 1], 1, f + 8)
                        load_b(wo[g * 4 + 2], 0, f + 9)
                        load_a(p, 5, g * 3 + 5)
                p = Pos(sp, b, 7)
                load_b(weff[6], 1, b40 + 34)
                load_a(p, 3, 0)
                load_b(wo[27], 0, b40 + 35)
                load_a(p, 4, 1)
                load_b(weff[7], 1, b40 + 36)
                load_b(wo[28], 0, b40 + 37)
                store_gate(b8, 6)
                load_b(wo[29], 1, b40 + 38)
                store_gate(b8, 7)
                load_b(wo[30], 0, b40 + 39)
                for i in range(2):
                    sp.wait_ge(gate_out[i], b * 64 + 64 + 16)
                for c in range(2):
                    sp.dma_start(g_buf[:, c, :], gate_dram[c]).then_inc(fin_in[c], 16)
                    sp.dma_start(x_buf[:, c, :], xT[bass.ds(b * 8 + c, 1)].rearrange(
                        "o p n -> (o p) n")).then_inc(fin_in[c], 16)
                load_b(wo[31], 1, b40 + 40)
                load_a(p, 5, 2)
                load_b(weff[0], 0, b40 + 41)
                load_b(weff[1], 1, b40 + 42)
                for c in range(NK):
                    sp.wait_ge(fin_done, b8 + c + 2)
                    sp.dma_start(outT[bass.ds(b * 8 + c, 1)].rearrange("o p n -> (o p) n"),
                                 acc[:, c, :]).then_inc(res_out[c % 2], 16)
                    if c + 2 < NK:
                        sp.dma_start(g_buf[:, c % 2, :], gate_dram[c + 2]).then_inc(fin_in[c % 2], 16)
                        sp.dma_start(x_buf[:, c % 2, :],
                                     xT[bass.ds(b * 8 + (c + 2), 1)].rearrange("o p n -> (o p) n")
                                     ).then_inc(fin_in[c % 2], 16)
            for i in range(2):
                sp.wait_ge(res_out[i], 64 * BATCH + 16)
                sp.wait_ge(gate_out[i], 64 * BATCH + 16)
            sp.wait_ge(x_in, 16 * (BATCH + 1))

        @block.tensor
        def _(pe):
            pe.nop().then_inc(po_done, PO_LEAD)
            pe.nop().then_inc(pv_done, 1)
            before = [None, None]
            turn = [0]

            def proj_bank(release):
                n = turn[0] % 2
                if before[n] is not None:
                    pe.wait_ge(*before[n])
                before[n] = release
                turn[0] += 1
                return proj_ps[n]

            def three(out, hi_l, lo_l, hi_r, lo_r, first, last):
                pe.matmul(out, hi_l, hi_r, start=first, stop=False)
                pe.matmul(out, hi_l, lo_r, start=False, stop=False)
                return pe.matmul(out, lo_l, hi_r, start=False, stop=last)

            def project(pos, tile, t):
                slot = tile_slot(pos, tile)
                bank = proj_bank((a_free, pos.at(12, 4 * tile + t + 1 + 1)))
                if t == 0:
                    pe.wait_ge(wa_ready, pos.at(6, 2 * tile + 2 + SLOT2))
                for k in range(NK):
                    cols = slice(t * P, t * P + P)
                    w = slice(k * 256, k * 256 + 256)
                    mm = three(bank[:, 0:256], xn_hi[:, k, cols], xn_lo[:, k, cols],
                               wa_hi[:, slot, w], wa_lo[:, slot, w], k == 0, k == NK - 1)
                mm.then_inc(a_done, 1)

            def gate(c, slot, pieces, number):
                bank = proj_bank((po_free, number + (1 + SLOT2)))
                pe.wait_ge(wb_ready, pieces)
                for k in range(NK):
                    w = slice(k * P, k * P + P)
                    mm = three(bank[:], wb_hi[:, slot, w], wb_lo[:, slot, w],
                               xn_hi[:, k, :], xn_lo[:, k, :], k == 0, k == NK - 1)
                mm.then_inc(po_done, 1)

            def out_proj(pair, slot, number, chunks):
                for c in chunks:
                    bank = proj_bank((po_free, number(c) + (1 + SLOT2)))
                    for hh in range(2):
                        w = slice(hh * 512 + c * P, hh * 512 + c * P + P)
                        mm = three(bank[:], wb_hi[:, slot, w], wb_lo[:, slot, w],
                                   o_hi[:, pair, hh, :], o_lo[:, pair, hh, :], hh == 0, hh == 1)
                    mm.then_inc(po_done, 1)

            def score_tile(pos, j, i):
                pe.wait_ge(scored, pos.at(16, 4 * j + i + 1))
                out = sc_ps[i % 2][:, 0:P * (i + 1)]
                q = slice(i * P, i * P + P)
                k = slice(0, P * (i + 1))
                three(out, qT_hi[:, j % 2, q], qT_lo[:, j % 2, q], kT_hi[:, k], kT_lo[:, k],
                      True, True).then_inc(s_done, 1)

            def attend(k):
                w = slice(PT_AT[k], PT_AT[k] + S - P * k)
                mm = three(ot_ps[:, P * k:S], v_hi[:, k, :], v_lo[:, k, :],
                           pT_hi[:, w], pT_lo[:, w], k == 0, k == NT - 1)
                if k == NT - 1:
                    mm.then_inc(pv_done, 1)

            def attend_ready(pos, j, before_bank):
                pe.wait_ge(tr_free, pos.tb(before_bank) + (1 + SLOT3))
                pe.wait_ge(ot_free, pos.at(4, j + 1))

            def turn_bank(pos, c):
                pe.wait_ge(tr_free, pos.tb(c) + (2 if c < 0 else 1))
                return tr_ps[(c + 1) % 3]

            def turn_probs(pos, c, key_tiles):
                for n, k in enumerate(key_tiles):
                    bank = turn_bank(pos, c + n)
                    for i in range(k, NT):
                        a = P_AT[i] + k * P
                        mm = pe.transpose(bank[:, i * P:i * P + P], prob[:, a:a + P], ident_sb[:])
                    mm.then_inc(tr_done, 1)

            def turn_rows(pos, rows, col, c, tile):
                pe.wait_ge(rows_ready, pos.at(3, tile + 1))
                bank = turn_bank(pos, c)
                for t in range(NT):
                    mm = pe.transpose(bank[:, t * P:t * P + P], rows[:, t, col:col + P], ident_sb[:])
                mm.then_inc(tr_done, 1)

            def turn_queries(pos, j, c):
                tile = {1: Q01, 2: Q23, 3: Q23, 4: 3 + Q01, 0: Q01}[j]
                turn_rows(pos, raw[tile % 3], (j % 2) * HD, c, tile)

            def turn_x(pos, c0):
                for c in range(NK):
                    bank = turn_bank(pos, c0 + c)
                    for t in range(NT):
                        mm = pe.transpose(bank[:, t * P:t * P + P], xtok[:, t, c * P:c * P + P],
                                          ident_sb[:])
                    mm.then_inc(tr_done, 1)

            pe.wait_ge(const_in, 16 * CONSTS)
            pe.wait_ge(ln_ready, 4)
            for c in range(NK):
                pe.wait_ge(tr_free, c + 1)
                for t in range(NT):
                    mm = pe.transpose(tr_ps[c % 3][:, t * P:t * P + P], xtok[:, t, c * P:c * P + P],
                                      ident_sb[:])
                mm.then_inc(tr_done, 1)
            pe.wait_ge(lora_ready, 4)
            for n in range(2 * NK):
                if n >= 2:
                    pe.wait_ge(weff_ready, n - 1)
                k, half = divmod(n, 2)
                a, o = slice(k * P, k * P + P), slice(half * 512, half * 512 + 512)
                three(proj_ps[n % 2][:], o_hi[:, 0].rearrange("p h s -> p (h s)")[:, a],
                      o_lo[:, 0].rearrange("p h s -> p (h s)")[:, a],
                      o_hi[:, 1].rearrange("p h s -> p (h s)")[:, o],
                      o_lo[:, 1].rearrange("p h s -> p (h s)")[:, o], True, True
                      ).then_inc(weff_done, 1)
            pe.wait_ge(weff_ready, 2 * NK)

            def tile_slot(pos, tile):
                return (pos.parity + tile) % 2

            def body(pos, gp, first, last):
                pos.parity = gp
                for j in range(G):
                    pe.wait_ge(tr_free, pos.tb(5 * j - 5 if j else -1) + (1 + SLOT3))
                    score_tile(pos, j, 0)
                    score_tile(pos, j, 1)
                    behind = not (first and j == 0)
                    if behind:
                        if j == 1:
                            pe.wait_ge(v_ready, pos.at(1, 1))
                        attend_ready(pos, j - 1, 5 * j - 1 if j else -3)
                        attend(0)
                    score_tile(pos, j, 2)
                    if behind:
                        attend(1)
                        attend(2)
                    score_tile(pos, j, 3)
                    if behind:
                        attend(3)
                    if j < 3:
                        turn_queries(pos, j + 1, 5 * j)
                    if first and j < 2:
                        gate(2 + 2 * j, 0, pos.at(0, 3 + 2 * j + SLOT2, 40), pos.first(2 + 2 * j))
                    if last and j in (1, 2):
                        gate(5 + j, 1, pos.at(4, 4 + 2 * j, 8) + SLOT2, pos.po(5 * j - 1))
                    for tile, t in PROJ[j]:
                        tile += 0 if tile == Q23 else 3
                        if last and tile != Q23:
                            continue
                        project(pos, tile, t)
                    if last and j == 3:
                        pe.wait_ge(ln_ready, pos.b * 4 + 8)
                        turn_x(pos, 15)
                    pair = 0 if j >= 2 else 1
                    slot, pieces, number = j % 2, pos.at(4, 5 + j, 8), lambda c: pos.po(4 * j + c)
                    if first:
                        number = lambda c: pos.first(4 * j - 2 + c)
                        pieces = pos.at(0, 5 + j, 40)
                    if last:
                        slot = [0, 0, 0, 1][j]
                        pieces = pos.at(4, [5, 7, 9, 10][j], 8)
                        number = lambda c: pos.po([0, 5, 10, 14][j] + c)
                    late_gate = first and j < 2
                    if not late_gate:
                        pe.wait_ge(wb_ready, pieces + SLOT2)
                        pe.wait_ge(ot_free, pos.at(4, 3 if j >= 2 else 1))
                        out_proj(pair, slot, number, (0, 1))
                    pe.wait_ge(prob_ready, pos.at(4, j + 1))
                    c = 5 * j + 1 if j < 3 else 23 if last else 15
                    turn_probs(pos, c, (0, 1, 2))
                    if late_gate:
                        gate(3 + 2 * j, 1, pos.at(0, 4 + 2 * j + SLOT2, 40), pos.first(3 + 2 * j))
                    else:
                        out_proj(pair, slot, number, (2,))
                    turn_probs(pos, c + 3, (3,))
                    if j == 3 and not last:
                        turn_rows(pos, raw[KV], 0, 19, 3 + KV)
                        turn_queries(pos, 4, 20)
                    if not late_gate:
                        out_proj(pair, slot, number, (3,))

            with pe.Fori(0, BATCH) as b:
                turn[0] = 0
                pos = Pos(pe, b, 0)
                pos.parity = 0
                before[0], before[1] = (po_free, pos.first(-1 + SLOT2)), (po_free, pos.first(SLOT2))
                pe.wait_ge(tr_free, pos.tb(-3) + (1 + SLOT3))
                for tile in (KV, Q01):
                    for t in range(NT):
                        project(pos, tile, t)
                gate(0, 0, pos.at(0, 1 + SLOT2, 40), pos.first(0))
                turn_rows(pos, raw[KV], 0, -2, KV)
                turn_queries(pos, 0, -1)
                gate(1, 1, pos.at(0, 2 + SLOT2, 40), pos.first(1))
                body(pos, 0, True, False)
                with pe.Fori(0, 3) as pair:
                    for h in range(2):
                        p = Pos(pe, b, pair * 2 + (1 + h))
                        before[0], before[1] = (po_free, p.po(-1 + SLOT2)), (po_free, p.po(SLOT2))
                        turn[0] = 0
                        body(p, (1 + h) % 2, False, False)
                p = Pos(pe, b, 7)
                before[0], before[1] = (po_free, p.po(-1 + SLOT2)), (po_free, p.po(SLOT2))
                turn[0] = 0
                body(p, 1, False, True)
                attend_ready(p, 3, 26)
                for k in range(NT):
                    attend(k)
                for j in range(2):
                    pe.wait_ge(wb_ready, p.at(4, 11 + j + SLOT2, 8))
                    if j == 0:
                        pe.wait_ge(ot_free, p.at(4, 4 + 1))
                    out_proj(1, j, lambda c: p.po(18 + 4 * j + c), range(4))

        @block.scalar
        def _(act):
            act.nop().then_inc(a_free, 1)
            act.wait_ge(const_in, 16 * CONSTS)
            act.preload_act_table_set("natural_log_exp_and_others")

            def split_a(pos, tile, parity, used):
                slot = (parity + tile) % 2
                for half in range(2):
                    act.wait_ge(a_in[half], pos.at(48, 16 * (tile + 1)))
                    if half == 0 and used is not None:
                        act.wait_ge(*used)
                    act.activation(wa_hi[:, slot, half * TILE:(half + 1) * TILE], stage_a[:, half, :],
                                   ACT.Copy).then_inc(wa_hi_done, 1)

            def split_b(slot, landed, used):
                act.wait_ge(b_in[slot], landed)
                act.wait_ge(po_done, used + PO_LEAD)
                act.activation(wb_hi[:, slot, :], stage_b[:, slot, :], ACT.Copy).then_inc(wb_hi_done, 1)

            def copy_rows(pos, tile, t):
                act.wait_ge(a_done, pos.at(12, 4 * tile + t + 1))
                act.activation(raw[tile % 3][:, t, :], proj_ps[turn[0] % 2][:, 0:256], ACT.Copy
                               ).then_inc(a_free, 1)

            def rsqrt(pos, tile, n):
                act.wait_ge(var_ready, pos.at(3, tile + 1))
                act.activation(lnv[:, 0:n], var[:, 0:n], ACT.Ln).then_inc(ln_done, 1)
                act.wait_ge(ln_done, pos.at(3, tile + 1))
                act.activation(rinv[:, 0:n], lnv[:, 0:n], ACT.Exp, scale=-0.5).then_inc(r0_done, 1)

            def take_hi(pos, c, dst, src=None, scale=1.0):
                act.wait_ge(tr_done, pos.tb(c) + 1)
                bank = tr_ps[(c + 1) % 3][:]
                act.activation(dst, bank if src is None else bank[:, src], ACT.Copy, scale=scale
                               ).then_inc(tr_hi, 1)

            def exps(pos, j):
                for i in range(NT):
                    act.wait_ge(scored, pos.at(16, 4 * j + i + 1 + SLOT2))
                    p = prob[:, P_AT[i]:P_AT[i] + P * (i + 1)]
                    act.activation(p, p, ACT.Exp, bias=negmax[:, i:i + 1], scale=-1.0,
                                   accum_out=rowsum[:, i:i + 1]).then_inc(exp_done, 1)

            def head_out(pos, j, pair, hh):
                act.wait_ge(pv_done, pos.at(4, j + 1 + 1))
                act.activation(o_hi[:, pair, hh, :], ot_ps[:], ACT.Copy).then_inc(ot_hi, 1)

            def gate_exp_of(pos, c, number):
                bank = turn[0] % 2
                turn[0] += 1
                act.wait_ge(po_done, number + (1 + PO_LEAD))
                if c < 2:
                    act.wait_ge(fin_done, pos.at(0, 1, 8))
                else:
                    act.wait_ge(gate_ready, pos.at(0, c - 1, 8))
                act.activation(g_buf[:, c % 2, :], proj_ps[bank][:], ACT.Exp, scale=-1.0,
                               bias=nfb[:, c:c + 1]).then_inc(gate_exp, 1)

            turn = [0]

            act.wait_ge(ln_var, 1)
            act.activation(lnv_x[:], var_x[:], ACT.Ln).then_inc(ln_log, 1)
            act.wait_ge(ln_log, 1)
            act.activation(rinv_x[:], lnv_x[:], ACT.Exp, scale=-0.5).then_inc(ln_r0, 1)
            act.wait_ge(lora_in, 32)
            act.activation(o_hi[:, 0].rearrange("p h s -> p (h s)"), stage_b[:, 0, :], ACT.Copy
                           ).then_inc(lora_hi, 1)
            act.wait_ge(lora_scaled, 1)
            act.activation(o_hi[:, 1].rearrange("p h s -> p (h s)"), stage_b[:, 1, :], ACT.Copy
                           ).then_inc(lora_hi, 1)
            for tile in (KV, Q01):
                for half in range(2):
                    act.wait_ge(a_in[half], 16 * (tile + 1))
                    act.activation(wa_hi[:, tile, half * TILE:(half + 1) * TILE],
                                   stage_a[:, half, :], ACT.Copy).then_inc(wa_hi_done, 1)
            for c in range(NK):
                act.wait_ge(tr_done, c + 1)
                act.activation(xn_hi[:, c, :], tr_ps[c % 3][:], ACT.Copy).then_inc(tr_hi, 1)

            def body(pos, gp, first, last):
                for j in range(G):
                    exps(pos, j)
                    if not (first and j == 0):
                        head_out(pos, j - 1, 0 if j in (1, 2) else 1, (j - 1) % 2)
                    if j < 3:
                        take_hi(pos, 5 * j, qT_hi[:, (j + 1) % 2, :])
                    if j == 0:
                        act.activation(v_hi[:], raw[KV][:, :, HD:2 * HD], ACT.Copy
                                       ).then_inc(v_hi_done, 1)
                    if first:
                        split_b(*[(1, pos.at(0, 32, 320), pos.first(2)),
                                  (1, pos.at(0, 48, 320), pos.first(4)),
                                  (1, pos.at(0, 64, 320), pos.first(6)),
                                  (0, pos.at(0, 80, 320), pos.first(10))][j])
                        if j < 2:
                            gate_exp_of(pos, 2 + 2 * j, pos.first(2 + 2 * j))
                            split_b(*[(0, pos.at(0, 48, 320), pos.first(3)),
                                      (0, pos.at(0, 64, 320), pos.first(5))][j])
                    elif last:
                        split_b(*[(1, pos.at(32, 48, 64), pos.po(0)),
                                  (0, pos.at(32, 64, 64), pos.po(4)),
                                  (0, pos.at(32, 80, 64), pos.po(9)),
                                  (0, pos.at(32, 96, 64), pos.po(14))][j])
                        if j in (1, 2):
                            gate_exp_of(pos, 5 + j, pos.po(5 * j - 1))
                            split_b(*[(1, pos.at(32, 64, 64), pos.po(5)),
                                      (1, pos.at(32, 80, 64), pos.po(10))][j - 1])
                    else:
                        split_b((j + 1) % 2, pos.at(32, 16 * ((5 + j) // 2 + 1), 64), pos.po(4 * j))
                    if j == 0:
                        split_a(pos, 3 + KV, gp, (a_done, pos.at(12, 8)))
                    for tile, t in PROJ[j]:
                        tile += 0 if tile == Q23 else 3
                        if last and tile != Q23:
                            continue
                        if t == 0 and tile % 3 == KV:
                            act.wait_ge(v_ready, pos.at(1, 1))
                        copy_rows(pos, tile, t)
                        turn[0] += 1
                        if t == 3:
                            rsqrt(pos, tile, 4 if tile % 3 == KV else 8)
                    if j == 1:
                        split_a(pos, 3 + Q01, gp, (a_done, pos.at(12, 12)))
                    if j == 3 and not last:
                        split_a(pos, 3 + Q23, gp, (a_done, pos.at(12, 16)))
                    if j == 3 and last:
                        for c in range(NK):
                            take_hi(pos, 15 + c, xn_hi[:, c, :])
                    if not (first and j < 2):
                        turn[0] += 4
                    c = 5 * j + 1 if j < 3 else 23 if last else 15
                    for k in range(NT):
                        w = slice(PT_AT[k], PT_AT[k] + S - P * k)
                        take_hi(pos, c + k, pT_hi[:, w], slice(P * k, S))
                    if j == 3 and not last:
                        take_hi(pos, 19, kT_hi[:], scale=qkw[:, 0:1])
                        take_hi(pos, 20, qT_hi[:, 0, :])
                    if first and j < 2:
                        gate_exp_of(pos, 3 + 2 * j, pos.first(3 + 2 * j))
                    if first and j == 1:
                        act.wait_ge(ln_var, pos.b + 2)
                        act.activation(lnv_x[:], var_x[:], ACT.Ln).then_inc(ln_log, 1)
                        act.wait_ge(ln_log, pos.b + 2)
                        act.activation(rinv_x[:], lnv_x[:], ACT.Exp, scale=-0.5).then_inc(ln_r0, 1)

            act.wait_ge(small_ready, 2)
            with act.Fori(0, BATCH) as b:
                turn[0] = 0
                pos = Pos(act, b, 0)
                split_b(0, pos.at(0, 16, 320), pos.first(-4))
                split_b(1, pos.at(0, 16, 320), pos.first(0))
                for t in range(NT):
                    copy_rows(pos, KV, t)
                    turn[0] += 1
                rsqrt(pos, KV, 4)
                split_a(pos, Q23, 0, (a_done, pos.at(12, 4)))
                for t in range(NT):
                    copy_rows(pos, Q01, t)
                    turn[0] += 1
                rsqrt(pos, Q01, 8)
                gate_exp_of(pos, 0, pos.first(0))
                split_b(0, pos.at(0, 32, 320), pos.first(1))
                take_hi(pos, -2, kT_hi[:], scale=qkw[:, 0:1])
                take_hi(pos, -1, qT_hi[:, 0, :])
                gate_exp_of(pos, 1, pos.first(1))
                body(pos, 0, True, False)
                with act.Fori(0, 3) as pair:
                    for h in range(2):
                        turn[0] = 0
                        body(Pos(act, b, pair * 2 + (1 + h)), (1 + h) % 2, False, False)
                turn[0] = 0
                p = Pos(act, b, 7)
                body(p, 1, False, True)
                head_out(p, 3, 1, 1)
                split_b(1, p.at(32, 96, 64), p.po(18))

        @block.gpsimd
        def _(pool):
            pool.nop().then_inc(wa_ready, SLOT2)
            pool.nop().then_inc(wb_ready, SLOT2)
            pool.nop().then_inc(fin_done, 1)
            pool.wait_ge(const_in, 16 * CONSTS)

            def low_a(pos, tile, parity):
                slot = (parity + tile) % 2
                for half in range(2):
                    w = slice(half * TILE, (half + 1) * TILE)
                    pool.wait_ge(wa_hi_done, pos.at(6, 2 * tile + half + 1))
                    pool.tensor_tensor(wa_lo[:, slot, w], stage_a[:, half, :], wa_hi[:, slot, w],
                                       ALU.subtract).then_inc(wa_ready, 1)

            def low_b(slot, made):
                pool.wait_ge(wb_hi_done, made)
                pool.tensor_tensor(wb_lo[:, slot, :], stage_b[:, slot, :], wb_hi[:, slot, :],
                                   ALU.subtract).then_inc(wb_ready, 1)

            def bias_of(pos, j):
                wait_alone(pool, scored, pos.at(16, 4 * j - 4 + SLOT2))
                pool.tensor_scalar(bias_sb[:, j % 2, :], rel_sb[:], slope[:, j % 4:j % 4 + 1], None,
                                   ALU.mult).then_inc(bias_ready, 1)

            pool.tensor_scalar(bias_sb[:, 0, :], rel_sb[:], slope[:, 0:1], None, ALU.mult
                               ).then_inc(bias_ready, 1)
            for tile in (KV, Q01):
                for half in range(2):
                    w = slice(half * TILE, (half + 1) * TILE)
                    pool.wait_ge(wa_hi_done, 2 * tile + half + 1)
                    pool.tensor_tensor(wa_lo[:, tile, w], stage_a[:, half, :], wa_hi[:, tile, w],
                                       ALU.subtract).then_inc(wa_ready, 1)

            def body(pos, gp, first, last):
                for j in range(G):
                    if j == 3:
                        wait_alone(pool, bias_ready, pos.at(4, 4))
                        if last:
                            pool.tensor_copy(slope[:], slope0[:]).then_inc(slope_ready, 1)
                        else:
                            pool.tensor_scalar(slope[:], slope[:], 0.5, None, ALU.mult
                                               ).then_inc(slope_ready, 1)
                        wait_alone(pool, slope_ready, pos.at(1, 1))
                    if first:
                        low_b([1, 1, 1, 0][j], pos.at(0, [4, 6, 8, 9][j], 40))
                    elif last:
                        low_b([1, 0, 0, 0][j], pos.at(4, [6, 7, 9, 11][j], 8))
                    else:
                        low_b((j + 1) % 2, pos.at(4, 6 + j, 8))
                    bias_of(pos, j + 1)
                    if first and j < 2:
                        low_b(0, pos.at(0, [5, 7][j], 40))
                    if last and j in (1, 2):
                        low_b(1, pos.at(4, [8, 10][j - 1], 8))
                    if j == 0:
                        low_a(pos, 3 + KV, gp)
                    if j == 1:
                        low_a(pos, 3 + Q01, gp)
                    if j == 3 and not last:
                        low_a(pos, 3 + Q23, gp)

            with pool.Fori(0, BATCH) as b:
                pos = Pos(pool, b, 0)
                low_b(0, pos.at(0, 1, 40))
                low_b(1, pos.at(0, 2, 40))
                low_a(pos, Q23, 0)
                low_b(0, pos.at(0, 3, 40))
                body(pos, 0, True, False)
                with pool.Fori(0, 3) as pair:
                    for h in range(2):
                        body(Pos(pool, b, pair * 2 + (1 + h)), (1 + h) % 2, False, False)
                p = Pos(pool, b, 7)
                body(p, 1, False, True)
                low_b(1, p.at(4, 12, 8))
                for c in range(NK):
                    pool.wait_ge(fin_in[c % 2], b * 128 + 32 * (c // 2 + 1))
                    pool.wait_ge(po_free, p.po(18 + c) + (1 + SLOT2))
                    pool.tensor_tensor(acc[:, c, :], g_buf[:, c % 2, :], acc[:, c, :],
                                       ALU.mult).then_inc(fin_step, 1)
                    pool.wait_ge(fin_step, b * 8 + (c + 1))
                    pool.tensor_tensor(acc[:, c, :], x_buf[:, c % 2, :], acc[:, c, :],
                                       ALU.add).then_inc(fin_done, 1)

        @block.vector
        def _(dve):
            dve.nop().then_inc(scored, SLOT2)
            dve.nop().then_inc(tr_free, SLOT3)
            dve.nop().then_inc(po_free, SLOT2)
            dve.nop().then_inc(ot_free, 1)
            dve.wait_ge(const_in, 16 * CONSTS)
            dve.tensor_tensor(qkw[:], qw_sb[:], kw_sb[:], ALU.mult).then_inc(small_ready, 1)
            dve.tensor_scalar(nfb[:], fb[:], -1.0, None, ALU.mult).then_inc(small_ready, 1)

            def newton_step(n, count, done, rinv, var, tmp):
                dve.tensor_tensor(tmp[:, 0:n], rinv[:, 0:n], rinv[:, 0:n], ALU.mult).then_inc(done, 1)
                dve.wait_ge(done, count(1))
                dve.tensor_tensor(tmp[:, 0:n], tmp[:, 0:n], var[:, 0:n], ALU.mult).then_inc(done, 1)
                dve.wait_ge(done, count(2))
                dve.tensor_scalar(tmp[:, 0:n], tmp[:, 0:n], -0.5, 1.5, ALU.mult, ALU.add
                                  ).then_inc(done, 1)
                dve.wait_ge(done, count(3))
                dve.tensor_tensor(rinv[:, 0:n], rinv[:, 0:n], tmp[:, 0:n], ALU.mult).then_inc(done, 1)
                dve.wait_ge(done, count(4))

            def layer_norm_stats(loaded, r):
                dve.wait_ge(x_in, loaded)
                for t in range(NT):
                    for i in range(2):
                        ins = dve.bn_stats(bn[:, t, 6 * i:6 * i + 6], xtok[:, t, 512 * i:512 * i + 512])
                ins.then_inc(ln_stat, 1)
                wait_alone(dve, ln_stat, r(2, 1))
                for t in range(NT):
                    ins = dve.bn_aggr(mv[:, t, :], bn[:, t, :])
                ins.then_inc(ln_stat, 1)
                dve.wait_ge(ln_stat, r(2, 2))
                dve.tensor_scalar(var_x[:], mv[:, :, 1], LN_EPS, None, ALU.add).then_inc(ln_var, 1)

            def layer_norm(r):
                dve.wait_ge(ln_r0, r(1, 1))
                newton_step(NT, lambda c: r(4, c), ln_newton, rinv_x, var_x, tmp_x)
                for t in range(NT):
                    dve.tensor_scalar(xtok[:, t, :], xtok[:, t, :], mv[:, t, 0:1], rinv_x[:, t:t + 1],
                                      ALU.subtract, ALU.mult).then_inc(ln_ready, 1)

            def row_stats(pos, tile, t):
                heads = 1 if tile % 3 == KV else 2
                dve.wait_ge(a_free, pos.at(12, 4 * tile + t + 1 + 1))
                for h in range(heads):
                    r = raw[tile % 3][:, t, h * HD:h * HD + HD]
                    at = t * heads + h
                    ins = dve.tensor_tensor_reduce(sq[:, at, :], r, r, 1.0, 0.0, ALU.mult, ALU.add,
                                                   ss[:, at:at + 1])
                if t == 3:
                    ins.then_inc(stat_ready, 1)

            def row_var(pos, tile):
                dve.wait_ge(stat_ready, pos.at(3, tile + 1))
                if tile % 3 == KV:
                    dve.tensor_scalar(var[:, 0:4], ss[:, 0:4], 1.0 / HD, RMS_EPS, ALU.mult, ALU.add
                                      ).then_inc(var_ready, 1)
                else:
                    dve.tensor_scalar(var[:], ss[:], HD * RMS_EPS, None, ALU.add
                                      ).then_inc(var_ready, 1)

            def scale_rows(pos, tile):
                n = 4 if tile % 3 == KV else 8
                dve.wait_ge(r0_done, pos.at(3, tile + 1))
                newton_step(n, lambda c: pos.at(12, 4 * tile + c), newton, rinv, var, tmp)
                if tile % 3 == KV:
                    r = raw[KV][:, :, 0:HD]
                    f = rinv[:, 0:4].unsqueeze(2).to_broadcast([P, NT, HD])
                else:
                    r = raw[tile % 3][:].rearrange("p t (h d) -> p (t h) d", h=2)
                    f = rinv[:].unsqueeze(2).to_broadcast([P, 8, HD])
                dve.tensor_tensor(r, r, f, ALU.mult).then_inc(rows_ready, 1)

            def take_lo(pos, c, dst, hi, src=None, scale=None):
                dve.wait_ge(tr_hi, pos.tb(c) + 1)
                bank = tr_ps[(c + 1) % 3][:]
                bank = bank if src is None else bank[:, src]
                if scale is None:
                    dve.tensor_tensor(dst, bank, hi, ALU.subtract).then_inc(tr_free, 1)
                else:
                    dve.scalar_tensor_tensor(out=dst, in0=bank, scalar=scale, in1=hi, op0=ALU.mult,
                                             op1=ALU.subtract).then_inc(tr_free, 1)

            def bias_and_max(pos, j):
                dve.wait_ge(bias_ready, pos.at(4, j + 1))
                for i in range(NT):
                    w = P * (i + 1)
                    wait_alone(dve, s_done, pos.at(16, 4 * j + i + 1))
                    dve.tensor_tensor_reduce(prob[:, P_AT[i]:P_AT[i] + w], sc_ps[i % 2][:, 0:w],
                                             bias_sb[:, j % 2, S - w:S], -1.0, 3e38,
                                             ALU.add, ALU.min, negmax[:, i:i + 1]).then_inc(scored, 1)

            def normalise(pos, j):
                dve.wait_ge(exp_done, pos.at(16, 4 * j + 4))
                dve.reciprocal(rs_inv[:], rowsum[:]).then_inc(rs_ready, 1)
                dve.wait_ge(rs_ready, pos.at(4, j + 1))
                for i in range(NT):
                    p = prob[:, P_AT[i]:P_AT[i] + P * (i + 1)]
                    ins = dve.tensor_scalar(p, p, rs_inv[:, i:i + 1], None, ALU.mult)
                ins.then_inc(prob_ready, 1)

            def head_out(pos, j, pair, hh):
                dve.wait_ge(ot_hi, pos.at(4, j + 1))
                dve.tensor_tensor(o_lo[:, pair, hh, :], ot_ps[:], o_hi[:, pair, hh, :], ALU.subtract
                                  ).then_inc(ot_free, 1)

            def add_out(number, chunk, copy):
                bank = turn[0]
                turn[0] += 1
                dve.wait_ge(po_done, number + (1 + PO_LEAD))
                if copy:
                    dve.tensor_copy(acc[:, chunk, :], proj_ps[bank % 2][:]).then_inc(po_free, 1)
                else:
                    dve.tensor_tensor(acc[:, chunk, :], acc[:, chunk, :], proj_ps[bank % 2][:],
                                      ALU.add).then_inc(po_free, 1)

            def gate(pos, c):
                bank = turn[0]
                turn[0] += 1
                e = g_buf[:, c % 2, :]
                dve.wait_ge(gate_exp, pos.at(0, c + 1, 8))
                dve.tensor_scalar(e, e, 1.0, None, ALU.add).then_inc(gate_step, 1)
                dve.wait_ge(gate_step, pos.at(0, 2 * c + 1, 16))
                dve.reciprocal(e, e).then_inc(gate_step, 1)
                dve.wait_ge(gate_step, pos.at(0, 2 * c + 2, 16))
                dve.wait_ge(gate_out[c % 2], pos.at(0, 16 * (c // 2) + 16, 64))
                dve.scalar_tensor_tensor(out=x_buf[:, c % 2, :], in0=proj_ps[bank % 2][:],
                                         scalar=fb[:, c:c + 1], in1=e, op0=ALU.add, op1=ALU.mult
                                         ).then_inc(gate_ready, 1)
                dve.wait_ge(gate_ready, pos.at(0, c + 1, 8))
                dve.nop().then_inc(po_free, 1)

            layer_norm_stats(16, lambda k, c: c)
            layer_norm(lambda k, c: c)
            dve.wait_ge(lora_in, 32)
            dve.tensor_scalar(stage_b[:, 1, :], stage_b[:, 1, :], lw_sb[:, 0:1], LORA_SCALE,
                              ALU.mult, ALU.mult).then_inc(lora_scaled, 1)
            for i in range(2):
                dve.wait_ge(lora_hi, i + 1)
                dve.tensor_tensor(o_lo[:, i].rearrange("p h s -> p (h s)"), stage_b[:, i, :],
                                  o_hi[:, i].rearrange("p h s -> p (h s)"), ALU.subtract
                                  ).then_inc(lora_ready, 2)
            for c in range(NK):
                dve.wait_ge(tr_hi, c + 1)
                dve.tensor_tensor(xn_lo[:, c, :], tr_ps[c % 3][:], xn_hi[:, c, :], ALU.subtract
                                  ).then_inc(tr_free, 1)
            for n in range(2 * NK):
                k, half = divmod(n, 2)
                dve.wait_ge(wt_in[k % 4], 16 * (k // 4 + 1))
                dve.wait_ge(weff_done, n + 1)
                w = acc[:, 2 * (k % 4) + half, :]
                dve.tensor_tensor(w, w, proj_ps[n % 2][:], ALU.add).then_inc(weff_ready, 1)

            turn = [0]

            def body(pos, gp, first, last):
                for j in range(G):
                    bias_and_max(pos, j)
                    normalise(pos, j)
                    if not (first and j == 0):
                        head_out(pos, j - 1, 0 if j in (1, 2) else 1, (j - 1) % 2)
                    if j < 3:
                        take_lo(pos, 5 * j, qT_lo[:, (j + 1) % 2, :], qT_hi[:, (j + 1) % 2, :])
                    if j == 0:
                        dve.wait_ge(v_hi_done, pos.at(1, 1))
                        dve.tensor_tensor(v_lo[:], raw[KV][:, :, HD:2 * HD], v_hi[:], ALU.subtract
                                          ).then_inc(v_ready, 1)
                    if first and j < 2:
                        gate(pos, 2 + 2 * j)
                    if last and j in (1, 2):
                        gate(pos, 5 + j)
                    groups = [(tile if tile == Q23 else tile + 3, t) for tile, t in PROJ[j]
                              if tile == Q23 or not last]
                    ended = None
                    for tile, t in groups:
                        row_stats(pos, tile, t)
                        turn[0] += 1
                        if t == 3:
                            row_var(pos, tile)
                            if (tile, t) != groups[-1]:
                                scale_rows(pos, tile)
                            else:
                                ended = tile
                    if last and j == 3:
                        for c in range(NK):
                            take_lo(pos, 15 + c, xn_lo[:, c, :], xn_hi[:, c, :])
                    if first and j == 1:
                        layer_norm_stats(pos.b * 16 + 32, lambda k, c: pos.b * k + (k + c))
                    if first and j == 2:
                        layer_norm(lambda k, c: pos.b * k + (k + c))
                        for i in range(2):
                            dve.wait_ge(res_out[i], pos.at(0, 16, 64))
                    adds = not (first and j < 2)
                    if first:
                        number = lambda c: pos.first(4 * j - 2 + c)
                    elif last:
                        number = lambda c: pos.po([0, 5, 10, 14][j] + c)
                    else:
                        number = lambda c: pos.po(4 * j + c)
                    half = 4 * (j % 2)
                    if adds:
                        for c in range(2):
                            add_out(number(c), half + c, first)
                    if ended is not None:
                        scale_rows(pos, ended)
                    c = 5 * j + 1 if j < 3 else 23 if last else 15

                    def probs_lo(k):
                        w = slice(PT_AT[k], PT_AT[k] + S - P * k)
                        take_lo(pos, c + k, pT_lo[:, w], pT_hi[:, w], slice(P * k, S))

                    for k in range(3):
                        probs_lo(k)
                    if adds:
                        add_out(number(2), half + 2, first)
                    probs_lo(3)
                    if j == 3 and not last:
                        take_lo(pos, 19, kT_lo[:], kT_hi[:], scale=qkw[:, 0:1])
                        take_lo(pos, 20, qT_lo[:, 0, :], qT_hi[:, 0, :])
                    if adds:
                        add_out(number(3), half + 3, first)
                    else:
                        gate(pos, 3 + 2 * j)

            with dve.Fori(0, BATCH) as b:
                turn[0] = 0
                pos = Pos(dve, b, 0)
                for tile in (KV, Q01):
                    for t in range(NT):
                        row_stats(pos, tile, t)
                        turn[0] += 1
                    row_var(pos, tile)
                    scale_rows(pos, tile)
                gate(pos, 0)
                take_lo(pos, -2, kT_lo[:], kT_hi[:], scale=qkw[:, 0:1])
                take_lo(pos, -1, qT_lo[:, 0, :], qT_hi[:, 0, :])
                gate(pos, 1)
                body(pos, 0, True, False)
                with dve.Fori(0, 3) as pair:
                    for h in range(2):
                        turn[0] = 0
                        body(Pos(dve, b, pair * 2 + (1 + h)), (1 + h) % 2, False, False)
                turn[0] = 0
                p = Pos(dve, b, 7)
                body(p, 1, False, True)
                head_out(p, 3, 1, 1)
                for c in range(NK):
                    add_out(p.po(18 + c), c, False)


def kernel(**inputs):
    import numpy as np
    import concourse.bacc as bacc
    from concourse.bass_utils import run_bass_kernel_spmd

    def f(name):
        return np.asarray(inputs[name])

    x = f("L0_attn_x")
    x_tok = x.reshape(BATCH, NT, P, D).transpose(0, 2, 1, 3)
    wq = f("L0_attn_Wq").T.reshape(2, 4, P, HKV, 2, 256)
    wk = f("L0_attn_Wk").T.reshape(2, 4, P, HKV, 1, HD)
    wv = f("L0_attn_Wv").T.reshape(2, 4, P, HKV, 1, HD)
    wkv = np.concatenate([wk, wv], axis=-1)
    wa = np.concatenate([wkv, wq], axis=4).transpose(3, 4, 0, 2, 1, 5).reshape(HKV * 6, P, TILE)
    wo = f("L0_attn_Wo").T.reshape(HKV, 2, 2, HD, 2, 512).transpose(0, 1, 4, 3, 2, 5)
    key = np.arange(S)[None, :] - np.arange(P)[:, None] - (S - P)
    start = 2.0 ** (-2.0 ** (-2.0))
    arrays = {
        "x_tok": np.roll(x_tok, -1, axis=0),
        "x_last": x_tok[0],
        "xT": x.transpose(0, 2, 1).reshape(BATCH * NK, P, S),
        "wa": wa,
        "wo": wo.reshape(HKV * 4, P, TILE),
        "wT": f("L0_ffn_W").T.reshape(NK, P, D),
        "lora_a": f("L0_ffn_lora_A").reshape(P, D),
        "lora_bt": f("L0_ffn_lora_B").transpose(0, 2, 1).reshape(P, D),
        "lw": f("L0_ffn_lora_weights").reshape(8, 1),
        "ffn_b": f("L0_ffn_bias").reshape(NK, P).T,
        "qw": f("L0_attn_q_norm_w").reshape(P, 1),
        "kw": f("L0_attn_k_norm_w").reshape(P, 1),
        "rel": np.where(key > 0, MASKED, key).astype(np.float32),
        "slopes": np.tile(np.array([start * start ** i for i in range(G)], np.float32), (P, 1)),
        "ident": np.eye(P, dtype=np.float32),
    }
    arrays = {k: np.ascontiguousarray(v) for k, v in arrays.items()}
    nc = bacc.Bacc("TRN2", target_bir_lowering=False, num_devices=1)
    args = [nc.dram_tensor(k, v.shape, F32, kind="ExternalInput").ap() for k, v in arrays.items()]
    outT = nc.dram_tensor("outT", (BATCH * NK, P, S), F32, kind="ExternalOutput").ap()
    build_layer(nc, *args, outT)
    got = run_bass_kernel_spmd(nc, [arrays], core_ids=[0]).results[0]["outT"]
    return np.ascontiguousarray(got.reshape(BATCH, D, S).transpose(0, 2, 1))
```

```python
from contextlib import ExitStack

import concourse.bass as bass
from concourse import mybir

ALU = mybir.AluOpType
ACT = mybir.ActivationFunctionType
F32 = mybir.dt.float32
F32R = mybir.dt.float32r

P = 128
BATCH, S, D = 4, 512, 1024
H, HKV, HD = 32, 8, 128
G = H // HKV
NT = S // P
NK = D // P
TILE = 1024
PW = P * NT * (NT + 1) // 2
RMS_EPS, LN_EPS = 1e-6, 1e-5
LORA_SCALE = 2.0
MASKED = -1e38

KV, Q01, Q23 = 0, 1, 2
PROJ = [[(Q23, t) for t in range(4)],
        [(KV, 0), (KV, 1), (KV, 2)],
        [(KV, 3), (Q01, 0), (Q01, 1)],
        [(Q01, 2), (Q01, 3)]]

P_AT = [P * i * (i + 1) // 2 for i in range(NT)]
PT_AT = [sum(S - P * m for m in range(k)) for k in range(NT)]

SLOT2 = 2
SLOT3 = 3
OUT_LEAD = 8
GATE_LEAD = 2
FIN_LEAD = NK


def held(eng, v):
    return v if isinstance(v, int) else eng.snap(v)


class Pos:

    def __init__(self, eng, b, g):
        self.eng, self.b, self.kept = eng, b, {}
        self.n = b * HKV + g

    def at(self, k, c, kb=0):
        if (k, kb) not in self.kept:
            v = self.n * k + self.b * kb if kb else self.n * k
            self.kept[k, kb] = held(self.eng, v)
        return self.kept[k, kb] + c

    def out(self, j, c):
        return self.at(16, 4 * j - 8 + c)

    def gate(self, c):
        return self.at(0, c, 8)

    def tb(self, c):
        return self.at(21, c + 10, 8)


def build_layer(nc, x_tok, x_first, xT, wa, wo, wT, lora_a, lora_bt, lw, ffn_b, qw, kw, rel, slopes,
                ident, outT):
    with ExitStack() as ctx:
        def sb(name, shape, dt=F32):
            return ctx.enter_context(nc.sbuf_tensor(name, shape, dt))

        def ps(name):
            return ctx.enter_context(nc.psum_tensor(name, [P, 512], F32))

        def sem(name):
            return ctx.enter_context(nc.semaphore(name))

        weff = nc.dram_tensor("weff", [NK, P, TILE], F32).ap()
        gate_dram = nc.dram_tensor("gate_dram", [NK, P, S], F32).ap()

        xtok = sb("xtok", [P, NT, D])
        xn_hi, xn_lo = sb("xn_hi", [P, NK, S], F32R), sb("xn_lo", [P, NK, S], F32R)
        acc = sb("acc", [P, NK, S])
        stage_a, stage_b = sb("stage_a", [P, 2, TILE]), sb("stage_b", [P, 2, TILE])
        wa_hi, wa_lo = sb("wa_hi", [P, 2, 2 * TILE], F32R), sb("wa_lo", [P, 2, 2 * TILE], F32R)
        wb_hi, wb_lo = sb("wb_hi", [P, 2, TILE], F32R), sb("wb_lo", [P, 2, TILE], F32R)
        raw = [sb("kv_raw", [P, NT, 256]), sb("q01_raw", [P, NT, 256]), sb("q23_raw", [P, NT, 256])]
        qT_hi, qT_lo = sb("qT_hi", [P, 2, S], F32R), sb("qT_lo", [P, 2, S], F32R)
        kT_hi, kT_lo = sb("kT_hi", [P, S], F32R), sb("kT_lo", [P, S], F32R)
        v_hi, v_lo = sb("v_hi", [P, NT, HD], F32R), sb("v_lo", [P, NT, HD], F32R)
        prob = sb("prob", [P, PW])
        pT_hi, pT_lo = sb("pT_hi", [P, PW], F32R), sb("pT_lo", [P, PW], F32R)
        bias_sb = sb("bias_sb", [P, 2, S])
        o_hi, o_lo = sb("o_hi", [P, 2, 2, S], F32R), sb("o_lo", [P, 2, 2, S], F32R)
        g_buf, x_buf = sb("g_buf", [P, 2, S]), sb("x_buf", [P, 2, S])
        ident_sb, rel_sb = sb("ident_sb", [P, P]), sb("rel_sb", [P, S])
        slope0, slope = sb("slope0", [P, G]), sb("slope", [P, G])
        qw_sb, kw_sb, qkw = sb("qw_sb", [P, 1]), sb("kw_sb", [P, 1]), sb("qkw", [P, 1])
        fb, lw_sb = sb("fb", [P, NK]), sb("lw_sb", [P, 1])
        sq = sb("sq", [P, 8, HD])
        ss, var, rinv, tmp = (sb(n, [P, 8]) for n in ("ss", "var", "rinv", "tmp"))
        lnv = sb("lnv", [P, 8])
        var_x, rinv_x, tmp_x, lnv_x = (sb(n, [P, NT]) for n in ("var_x", "rinv_x", "tmp_x", "lnv_x"))
        negmax, rowsum, rs_inv = (sb(n, [P, NT]) for n in ("negmax", "rowsum", "rs_inv"))
        bn = sb("bn", [P, NT, 12])
        mv = sb("mv", [P, NT, 2])

        proj_ps = [ps("proj0"), ps("proj1")]
        sc_ps = [ps("sc0"), ps("sc1")]
        tr_ps = [ps("tr0"), ps("tr1"), ps("tr2")]
        ot_ps = ps("ot")
        merge_ps = [sc_ps[0], sc_ps[1], ot_ps]

        const_in = sem("const_in")
        x_in = sem("x_in")
        a_in = [sem("a_in0"), sem("a_in1")]
        b_in = [sem("b_in0"), sem("b_in1")]
        x0_in = [sem(f"x0_in{t}") for t in range(NT)]
        lw_in = sem("lw_in")
        wt_in = [sem(f"wt_in{k}") for k in range(NK)]
        weff_out = sem("weff_out")
        gate_out = [sem("gate_out0"), sem("gate_out1")]
        fin_in = [sem(f"fin_in{c}") for c in range(NK)]
        res_out = [sem("res_out0"), sem("res_out1")]
        a_done = sem("a_done")
        out_done = sem("out_done")
        gate_done = sem("gate_done")
        s_done = sem("s_done")
        tr_done = sem("tr_done")
        pv_done = sem("pv_done")
        weff_done = sem("weff_done")
        a_free = sem("a_free")
        wa_hi_done, wb_hi_done = sem("wa_hi_done"), sem("wb_hi_done")
        exp_done = sem("exp_done")
        tr_hi = sem("tr_hi")
        ot_hi = sem("ot_hi")
        v_hi_done = sem("v_hi_done")
        ln_done, r0_done = sem("ln_done"), sem("r0_done")
        gate_free = sem("gate_free")
        gate_exp = sem("gate_exp")
        lora_hi = sem("lora_hi")
        merged_hi = sem("merged_hi")
        wa_ready, wb_ready = sem("wa_ready"), sem("wb_ready")
        bias_ready = sem("bias_ready")
        slope_ready = sem("slope_ready")
        fin_step, fin_done = sem("fin_step"), sem("fin_done")
        scored = sem("scored")
        rs_ready = sem("rs_ready")
        prob_ready = sem("prob_ready")
        tr_free = sem("tr_free")
        ot_free = sem("ot_free")
        v_ready = sem("v_ready")
        stat_ready = sem("stat_ready")
        var_ready = sem("var_ready")
        newton = sem("newton")
        rows_ready = sem("rows_ready")
        odd_ready = sem("odd_ready")
        out_free = sem("out_free")
        gate_step, gate_ready = sem("gate_step"), sem("gate_ready")
        qkw_ready = sem("qkw_ready")
        lora_ready = sem("lora_ready")
        lora_scaled = sem("lora_scaled")
        weff_ready = sem("weff_ready")
        ln_stat, ln_newton, ln_ready = sem("ln_stat"), sem("ln_newton"), sem("ln_ready")
        ln_var = sem("ln_var")
        ln_log, ln_r0 = sem("ln_log"), sem("ln_r0")

        passed = sem("passed")

        CONSTS = 6

        def gate_rows(k):
            if k < NT:
                return acc[:, 2 * k:2 * k + 2, :].rearrange("p a n -> p (a n)")
            return xtok[:, k - NT, :]

        def gate_tile(c, part):
            if part == 1:
                return xtok[:, :, c * P:c * P + P]
            rows = acc[:].rearrange("p (k a) n -> p k a n", a=2)
            return rows[:, :, c // 4, c % 4 * P:c % 4 * P + P]

        gate_at, x_at = [], []
        for buf in [raw[t][:].rearrange("p t w -> p (t w)") for t in (KV, Q01, Q23)] + [
                xtok[:, t, :] for t in range(NT)]:
            gate_at.append(buf[:, 0:S])
            x_at.append(buf[:, S:2 * S])
        gate_at.append(x_buf[:, 1, :])
        x_at.append(g_buf[:, 0, :])

        def wait_alone(eng, semaphore, value):
            eng.wait_ge(semaphore, value)
            eng.nop().then_inc(passed, 1)

        block = ctx.enter_context(nc.Block())

        @block.sync
        def _(sp):
            sp.nop().then_inc(gate_out[0], 16)
            sp.nop().then_inc(gate_out[1], 16)
            sp.nop().then_inc(res_out[0], 16)
            sp.nop().then_inc(res_out[1], 16)
            sp.dma_start(xtok[:, 0, :], x_first[:, 0, :]).then_inc(x0_in[0], 16)
            sp.dma_start(ident_sb[:], ident).then_inc(const_in, 16)
            for t in range(1, NT):
                sp.dma_start(xtok[:, t, :], x_first[:, t, :]).then_inc(x0_in[t], 16)
            for half in range(2):
                sp.dma_start(stage_a[:, half, :], wa[half]).then_inc(a_in[half], 16)
            for dst, src in ((rel_sb, rel), (slope0, slopes), (slope, slopes), (qw_sb, qw),
                             (kw_sb, kw)):
                sp.dma_start(dst[:], src).then_inc(const_in, 16)
            sp.dma_start(stage_b[:, 0, :], lora_a).then_inc(b_in[0], 16)
            sp.dma_start(stage_b[:, 1, :], lora_bt).then_inc(b_in[1], 16)
            sp.dma_start(fb[:], ffn_b).then_inc(lw_in, 16)
            for n in range(8):
                sp.dma_start(lw_sb[16 * n:16 * n + 16, :],
                             lw[n:n + 1, :].to_broadcast([16, 1])).then_inc(lw_in, 16)

            def load_a(pos, tile, dram):
                for half in range(2):
                    sp.wait_ge(wa_ready, pos.at(6, 2 * tile + half + 1))
                    sp.dma_start(stage_a[:, half, :], wa[dram * 2 + half]).then_inc(a_in[half], 16)

            def load_b(src, slot, free):
                sp.wait_ge(wb_ready, free)
                sp.dma_start(stage_b[:, slot, :], src).then_inc(b_in[slot], 16)

            def store_gate(b8, c):
                sp.wait_ge(gate_ready, b8 + (c + 1))
                sp.dma_start(gate_dram[c], x_buf[:, c % 2, :]).then_inc(gate_out[c % 2], 16)

            for half in range(2):
                sp.wait_ge(wa_ready, SLOT2 + half + 1)
                sp.dma_start(stage_a[:, half, :], wa[2 + half]).then_inc(a_in[half], 16)
            for k in range(NK):
                if k == NT:
                    sp.wait_ge(tr_done, NK)
                sp.dma_start(gate_rows(k), wT[k]).then_inc(wt_in[k], 16)
            load_a(Pos(sp, 0, 0), Q23, 2)
            for k in range(NK):
                sp.wait_ge(weff_ready, 2 * k + 2)
                sp.dma_start(weff.rearrange("c d (k o) -> d c k o", k=NK)[:, :, k, :],
                             gate_rows(k).rearrange("p (c o) -> p c o", o=P)
                             ).then_inc(weff_out, 16)
            sp.wait_ge(weff_out, 16 * NK)

            def load_result(stored, b8, c, after=None):
                if after is not None:
                    sp.wait_ge(*after)
                sp.dma_start(x_at[c], xT[bass.ds(b8 + c, 1)].rearrange("o p n -> (o p) n")
                             ).then_inc(fin_in[c], 16)
                if c < NK - 1:
                    sp.wait_ge(gate_out[c % 2], stored[c % 2] + (16 * (c // 2) + 32))
                    sp.dma_start(gate_at[c], gate_dram[c]).then_inc(fin_in[c], 16)

            def batch(b, opening):
                pos = Pos(sp, b, 0)
                b8, b40 = held(sp, b * 8), held(sp, b * 40)
                if not opening:
                    load_b(weff[0], 0, b40 + 1)
                    load_a(pos, Q23, 2)
                    load_b(weff[1], 1, b40 + 2)
                load_b(weff[2], 0, b40 + 3)
                load_b(weff[3], 1, b40 + 4)
                sp.wait_ge(tr_done, pos.tb(-2))
                sp.dma_start(xtok[:], x_tok[bass.ds(b, 1)].rearrange("o p t d -> (o p) t d")
                             ).then_inc(x_in, 16)
                load_b(weff[4], 0, b40 + 5)
                load_a(pos, 3, 3)
                store_gate(b8, 0)
                load_b(weff[5], 1, b40 + 6)
                store_gate(b8, 1)
                load_b(wo[0], 0, b40 + 7)
                load_a(pos, 4, 4)
                store_gate(b8, 2)
                load_b(wo[1], 1, b40 + 8)
                store_gate(b8, 3)
                load_b(wo[2], 0, b40 + 9)
                load_a(pos, 5, 5)
                store_gate(b8, 4)

                with sp.Fori(0, 3) as pair:
                    for h in range(2):
                        g = sp.snap(pair * 2 + (1 + h))
                        p, f = Pos(sp, b, g), sp.snap(b * 40 + g * 4)
                        load_b(wo[g * 4 - 1], 1, f + 6)
                        load_a(p, 3, g * 3 + 3)
                        load_b(wo[g * 4], 0, f + 7)
                        load_a(p, 4, g * 3 + 4)
                        load_b(wo[g * 4 + 1], 1, f + 8)
                        load_b(wo[g * 4 + 2], 0, f + 9)
                        load_a(p, 5, g * 3 + 5)
                p = Pos(sp, b, 7)
                stored = [held(sp, b * 64), held(sp, b * 48)]
                load_b(weff[6], 1, b40 + 34)
                load_a(p, 3, 0)
                load_b(wo[27], 0, b40 + 35)
                load_a(p, 4, 1)
                load_b(weff[7], 1, b40 + 36)
                store_gate(b8, 5)
                load_b(wo[28], 0, b40 + 37)
                load_b(wo[29], 1, b40 + 38)
                load_result(stored, b8, 0, (v_ready, p.at(1, 1)))
                load_result(stored, b8, 1, (tr_done, p.tb(0) + 1))
                load_b(wo[30], 0, b40 + 39)
                store_gate(b8, 6)
                load_b(wo[31], 1, b40 + 40)
                load_result(stored, b8, 2, (tr_done, p.tb(10) + 1))
                load_result(stored, b8, 3, (tr_done, p.tb(22) + 1))
                for c in range(4, NK):
                    load_result(stored, b8, c)
                for c in range(NK):
                    sp.wait_ge(fin_done, b8 + (c + 1 + FIN_LEAD))
                    sp.dma_start(outT[bass.ds(b8 + c, 1)].rearrange("o p n -> (o p) n"),
                                 acc[:, c, :]).then_inc(res_out[c % 2], 16)
            batch(0, True)
            with sp.Fori(1, BATCH) as b:
                batch(b, False)
            for i in range(2):
                sp.wait_ge(res_out[i], 64 * BATCH + 16)
                sp.wait_ge(gate_out[i], [64, 48][i] * BATCH + 16)
            sp.wait_ge(x_in, 16 * BATCH)

        @block.tensor
        def _(pe):
            pe.nop().then_inc(out_done, OUT_LEAD)
            pe.nop().then_inc(gate_done, GATE_LEAD)
            pe.nop().then_inc(pv_done, 1)
            before = [None, None]
            turn = [0]

            def proj_bank(release):
                n = turn[0] % 2
                if before[n] is not None:
                    pe.wait_ge(*before[n])
                before[n] = release
                turn[0] += 1
                return proj_ps[n]

            def three(out, hi_l, lo_l, hi_r, lo_r, first, last):
                pe.matmul(out, hi_l, hi_r, start=first, stop=False)
                pe.matmul(out, hi_l, lo_r, start=False, stop=False)
                return pe.matmul(out, lo_l, hi_r, start=False, stop=last)

            def project(pos, tile, t):
                slot = tile_slot(pos, tile)
                bank = proj_bank((a_free, pos.at(12, 4 * tile + t + 1 + 1)))
                if t == 0:
                    pe.wait_ge(wa_ready, pos.at(6, 2 * tile + 2 + SLOT2))
                for k in range(NK):
                    cols = slice(t * P, t * P + P)
                    w = slice(k * 256, k * 256 + 256)
                    mm = three(bank[:, 0:256], xn_hi[:, k, cols], xn_lo[:, k, cols],
                               wa_hi[:, slot, w], wa_lo[:, slot, w], k == 0, k == NK - 1)
                mm.then_inc(a_done, 1)

            def gate(pos, c, slot, pieces):
                bank = proj_bank((gate_free, pos.gate(c + 1)))
                pe.wait_ge(wb_ready, pieces)
                for k in range(NK):
                    w = slice(k * P, k * P + P)
                    mm = three(bank[:], wb_hi[:, slot, w], wb_lo[:, slot, w],
                               xn_hi[:, k, :], xn_lo[:, k, :], k == 0, k == NK - 1)
                mm.then_inc(gate_done, 1)

            def out_proj(pos, j, pair, slot, chunks):
                for c in chunks:
                    bank = proj_bank((out_free, pos.out(j, c + 1 + SLOT2)))
                    for hh in range(2):
                        w = slice(hh * 512 + c * P, hh * 512 + c * P + P)
                        mm = three(bank[:], wb_hi[:, slot, w], wb_lo[:, slot, w],
                                   o_hi[:, pair, hh, :], o_lo[:, pair, hh, :], hh == 0, hh == 1)
                    mm.then_inc(out_done, 1)

            def score_tile(pos, j, i):
                pe.wait_ge(scored, pos.at(16, 4 * j + i + 1))
                out = sc_ps[i % 2][:, 0:P * (i + 1)]
                q = slice(i * P, i * P + P)
                k = slice(0, P * (i + 1))
                three(out, qT_hi[:, j % 2, q], qT_lo[:, j % 2, q], kT_hi[:, k], kT_lo[:, k],
                      True, True).then_inc(s_done, 1)

            def attend(k):
                w = slice(PT_AT[k], PT_AT[k] + S - P * k)
                mm = three(ot_ps[:, P * k:S], v_hi[:, k, :], v_lo[:, k, :],
                           pT_hi[:, w], pT_lo[:, w], k == 0, k == NT - 1)
                if k == NT - 1:
                    mm.then_inc(pv_done, 1)

            def attend_ready(pos, j, before_bank):
                pe.wait_ge(tr_free, pos.tb(before_bank) + (1 + SLOT3))
                pe.wait_ge(ot_free, pos.at(4, j + 1))

            def turn_bank(pos, c):
                pe.wait_ge(tr_free, pos.tb(c) + (2 if c < 0 else 1))
                return tr_ps[(c + 1) % 3]

            def turn_probs(pos, c, key_tiles):
                for n, k in enumerate(key_tiles):
                    bank = turn_bank(pos, c + n)
                    for i in range(k, NT):
                        a = P_AT[i] + k * P
                        mm = pe.transpose(bank[:, i * P:i * P + P], prob[:, a:a + P], ident_sb[:])
                    mm.then_inc(tr_done, 1)

            def turn_rows(pos, rows, odd, c, tile):
                if odd:
                    pe.wait_ge(odd_ready, pos.at(2, 1 if tile == Q01 else 2))
                else:
                    pe.wait_ge(rows_ready, pos.at(3, tile + 1))
                col = odd * HD
                bank = turn_bank(pos, c)
                for t in range(NT):
                    mm = pe.transpose(bank[:, t * P:t * P + P], rows[:, t, col:col + P], ident_sb[:])
                mm.then_inc(tr_done, 1)

            def turn_queries(pos, j, c):
                tile = {1: Q01, 2: Q23, 3: Q23, 4: 3 + Q01, 0: Q01}[j]
                turn_rows(pos, raw[tile % 3], j % 2, c, tile)

            def turn_x(pos, c0, chunks):
                for c in chunks:
                    bank = turn_bank(pos, c0 + c)
                    for t in range(NT):
                        mm = pe.transpose(bank[:, t * P:t * P + P], xtok[:, t, c * P:c * P + P],
                                          ident_sb[:])
                    mm.then_inc(tr_done, 1)

            pe.wait_ge(const_in, 16 * CONSTS)
            for c in range(2 * NT):
                t, half = divmod(c, 2)
                pe.wait_ge(ln_ready, t + 1)
                pe.wait_ge(tr_free, c + 1)
                for i in range(4):
                    k = 4 * half + i
                    mm = pe.transpose(tr_ps[c % 3][:, i * P:i * P + P], xtok[:, t, k * P:k * P + P],
                                      ident_sb[:])
                mm.then_inc(tr_done, 1)

            def merge_gate():
                pe.wait_ge(lora_ready, 4)
                for n in range(2 * NK):
                    if n >= 3:
                        pe.wait_ge(weff_ready, n - 2)
                    bank = merge_ps[n % 3]
                    k, half = divmod(n, 2)
                    a, o = slice(k * P, k * P + P), slice(half * 512, half * 512 + 512)
                    three(bank[:], o_hi[:, 0].rearrange("p h s -> p (h s)")[:, a],
                          o_lo[:, 0].rearrange("p h s -> p (h s)")[:, a],
                          o_hi[:, 1].rearrange("p h s -> p (h s)")[:, o],
                          o_lo[:, 1].rearrange("p h s -> p (h s)")[:, o], True, True
                          ).then_inc(weff_done, 1)

            def tile_slot(pos, tile):
                return (pos.parity + tile) % 2

            def body(pos, gp, first, last):
                pos.parity = gp
                for j in range(G):
                    pe.wait_ge(tr_free, pos.tb(5 * j - 5 if j else -1 if first else -2) + (1 + SLOT3))
                    score_tile(pos, j, 0)
                    score_tile(pos, j, 1)
                    behind = not (first and j == 0)
                    if behind:
                        if j == 1:
                            pe.wait_ge(v_ready, pos.at(1, 1))
                        attend_ready(pos, j - 1, 5 * j - 2 if j else -3)
                        attend(0)
                    score_tile(pos, j, 2)
                    if behind:
                        attend(1)
                        attend(2)
                    score_tile(pos, j, 3)
                    if behind:
                        pe.wait_ge(tr_free, pos.tb(5 * j - 1) + (1 + SLOT3))
                        attend(3)
                    if j < 3:
                        turn_queries(pos, j + 1, 5 * j)
                    elif not last:
                        turn_rows(pos, raw[KV], 0, 15, 3 + KV)
                    if first and j < 2:
                        gate(pos, 2 + 2 * j, 0, pos.at(0, 3 + 2 * j + SLOT2, 40))
                    if last and j in (1, 2):
                        gate(pos, 5 + j, 1, pos.at(4, 4 + 2 * j, 8) + SLOT2)
                    for tile, t in PROJ[j]:
                        tile += 0 if tile == Q23 else 3
                        if last and tile != Q23:
                            continue
                        project(pos, tile, t)
                    pair = 0 if j >= 2 else 1
                    slot, pieces = j % 2, pos.at(4, 5 + j, 8)
                    if first:
                        pieces = pos.at(0, 5 + j, 40)
                    if last:
                        slot, pieces = [0, 0, 0, 1][j], pos.at(4, [5, 7, 9, 10][j], 8)
                    late_gate = first and j < 2
                    if last and j == 3:
                        turn_x(pos, 15, (2, 3, 4))
                        pe.wait_ge(wb_ready, pieces + SLOT2)
                        out_proj(pos, j, pair, slot, (0,))
                        turn_x(pos, 15, (5, 6, 7))
                        out_proj(pos, j, pair, slot, (1,))
                        pe.wait_ge(prob_ready, pos.at(4, j + 1))
                        turn_probs(pos, 23, (0, 1, 2))
                        out_proj(pos, j, pair, slot, (2,))
                        turn_probs(pos, 26, (3,))
                        continue
                    if not late_gate:
                        pe.wait_ge(wb_ready, pieces + SLOT2)
                        pe.wait_ge(ot_free, pos.at(4, 3 if j >= 2 else 1))
                        out_proj(pos, j, pair, slot, (0, 1))
                    pe.wait_ge(prob_ready, pos.at(4, j + 1))
                    c = 23 if last and j == 3 else 5 * j + 1
                    turn_probs(pos, c, (0, 1, 2))
                    if late_gate:
                        gate(pos, 3 + 2 * j, 1, pos.at(0, 4 + 2 * j + SLOT2, 40))
                    else:
                        out_proj(pos, j, pair, slot, (2,))
                    if j == 3 and not last:
                        turn_queries(pos, 4, 19)
                        c += 1
                    turn_probs(pos, c + 3, (3,))
                    if last and j == 2:
                        pe.wait_ge(ln_ready, pos.b * 4 + 8)
                        turn_x(pos, 15, (0, 1))
                    if not late_gate:
                        out_proj(pos, j, pair, slot, (3,))

            def batch(b, opening):
                turn[0] = 0
                pos = Pos(pe, b, 0)
                pos.parity = 0
                before[0], before[1] = (out_free, pos.out(2, -1 + SLOT2)), (out_free, pos.out(2, SLOT2))
                if not opening:
                    pe.wait_ge(tr_free, pos.tb(-3) + (1 + SLOT3))
                for t in range(NT):
                    if opening:
                        pe.wait_ge(tr_free, 2 * t + 2 + SLOT3)
                    project(pos, KV, t)
                if opening:
                    merge_gate()
                for t in range(NT):
                    project(pos, Q01, t)
                if opening:
                    pe.wait_ge(weff_ready, 2 * NK)
                gate(pos, 0, 0, pos.at(0, 1 + SLOT2, 40))
                turn_rows(pos, raw[KV], 0, -2, KV)
                turn_queries(pos, 0, -1)
                gate(pos, 1, 1, pos.at(0, 2 + SLOT2, 40))
                body(pos, 0, True, False)
                with pe.Fori(0, 3) as pair:
                    for h in range(2):
                        p = Pos(pe, b, pair * 2 + (1 + h))
                        before[0], before[1] = (out_free, p.out(0, -1 + SLOT2)), (out_free, p.out(0, SLOT2))
                        turn[0] = 0
                        body(p, (1 + h) % 2, False, False)
                p = Pos(pe, b, 7)
                before[0], before[1] = (out_free, p.out(0, -1 + SLOT2)), (out_free, p.out(0, SLOT2))
                turn[0] = 0
                body(p, 1, False, True)
                attend_ready(p, 3, 25)
                for k in range(NT):
                    if k == NT - 1:
                        pe.wait_ge(tr_free, p.tb(26) + (1 + SLOT3))
                    attend(k)
                out_proj(p, 3, 0, 1, (3,))
                for j in range(2):
                    pe.wait_ge(wb_ready, p.at(4, 11 + j + SLOT2, 8))
                    if j == 0:
                        pe.wait_ge(ot_free, p.at(4, 4 + 1))
                    out_proj(p, 4 + j, 1, j, range(4))

            batch(0, True)
            with pe.Fori(1, BATCH) as b:
                batch(b, False)

        @block.scalar
        def _(act):
            act.nop().then_inc(a_free, 1)
            act.preload_act_table_set("natural_log_exp_and_others")

            def split_a(pos, tile, parity, used, halves=(0, 1)):
                slot = (parity + tile) % 2
                for half in halves:
                    act.wait_ge(a_in[half], pos.at(48, 16 * (tile + 1)))
                    if half == 0 and used is not None:
                        act.wait_ge(*used)
                    act.activation(wa_hi[:, slot, half * TILE:(half + 1) * TILE], stage_a[:, half, :],
                                   ACT.Copy).then_inc(wa_hi_done, 1)

            def out_used(pos, j):
                return out_done, pos.out(j, 4 + OUT_LEAD)

            def gate_used(pos, c):
                return gate_done, pos.gate(c + 1 + GATE_LEAD)

            def split_b(slot, landed, used):
                act.wait_ge(b_in[slot], landed)
                act.wait_ge(*used)
                act.activation(wb_hi[:, slot, :], stage_b[:, slot, :], ACT.Copy).then_inc(wb_hi_done, 1)

            def copy_rows(pos, tile, t):
                act.wait_ge(a_done, pos.at(12, 4 * tile + t + 1))
                act.activation(raw[tile % 3][:, t, :], proj_ps[turn[0] % 2][:, 0:256], ACT.Copy
                               ).then_inc(a_free, 1)

            def rsqrt(pos, tile, n):
                act.wait_ge(var_ready, pos.at(3, tile + 1))
                act.activation(lnv[:, 0:n], var[:, 0:n], ACT.Ln).then_inc(ln_done, 1)
                act.wait_ge(ln_done, pos.at(3, tile + 1))
                act.activation(rinv[:, 0:n], lnv[:, 0:n], ACT.Exp, scale=-0.5).then_inc(r0_done, 1)

            def take_hi(pos, c, dst, src=None, scale=1.0):
                act.wait_ge(tr_done, pos.tb(c) + 1)
                bank = tr_ps[(c + 1) % 3][:]
                act.activation(dst, bank if src is None else bank[:, src], ACT.Copy, scale=scale
                               ).then_inc(tr_hi, 1)

            def exps(pos, j):
                for i in range(NT):
                    act.wait_ge(scored, pos.at(16, 4 * j + i + 1 + SLOT2))
                    p = prob[:, P_AT[i]:P_AT[i] + P * (i + 1)]
                    act.activation(p, p, ACT.Exp, bias=negmax[:, i:i + 1], scale=-1.0,
                                   accum_out=rowsum[:, i:i + 1]).then_inc(exp_done, 1)

            def head_out(pos, j, pair, hh):
                act.wait_ge(pv_done, pos.at(4, j + 1 + 1))
                act.activation(o_hi[:, pair, hh, :], ot_ps[:], ACT.Copy).then_inc(ot_hi, 1)

            def gate_exp_of(pos, c):
                bank = turn[0] % 2
                turn[0] += 1
                act.wait_ge(gate_done, pos.gate(c + 1 + GATE_LEAD))
                if c < 2:
                    act.wait_ge(fin_done, pos.gate(FIN_LEAD))
                else:
                    act.wait_ge(gate_ready, pos.gate(c - 1))
                act.wait_ge(gate_out[c % 2], pos.at(0, 16 * (c // 2) + 16, [64, 48][c % 2]))
                act.activation(x_buf[:, c % 2, :], proj_ps[bank][:], ACT.Identity,
                               bias=fb[:, c:c + 1]).then_inc(gate_free, 1)
                act.wait_ge(gate_free, pos.gate(c + 1))
                act.activation(g_buf[:, c % 2, :], x_buf[:, c % 2, :], ACT.Exp, scale=-1.0
                               ).then_inc(gate_exp, 1)

            turn = [0]

            act.wait_ge(ln_var, 1)
            act.activation(lnv_x[:], var_x[:], ACT.Ln).then_inc(ln_log, 1)
            act.wait_ge(ln_log, 1)
            act.activation(rinv_x[:], lnv_x[:], ACT.Exp, scale=-0.5).then_inc(ln_r0, 1)

            def first_a(tile, half):
                act.wait_ge(a_in[half], 16 * (tile + 1))
                act.activation(wa_hi[:, tile, half * TILE:(half + 1) * TILE],
                               stage_a[:, half, :], ACT.Copy).then_inc(wa_hi_done, 1)

            first_a(KV, 0)
            first_a(KV, 1)
            for c in range(2 * NT):
                t, half = divmod(c, 2)
                act.wait_ge(tr_done, c + 1)
                act.activation(xn_hi[:, 4 * half:4 * half + 4, t * P:t * P + P],
                               tr_ps[c % 3][:].rearrange("p (k o) -> p k o", o=P), ACT.Copy
                               ).then_inc(tr_hi, 1)
            act.wait_ge(b_in[0], 16)
            act.activation(o_hi[:, 0].rearrange("p h s -> p (h s)"), stage_b[:, 0, :], ACT.Copy
                           ).then_inc(lora_hi, 1)
            act.wait_ge(lora_scaled, 1)
            act.activation(o_hi[:, 1].rearrange("p h s -> p (h s)"), stage_b[:, 1, :], ACT.Copy
                           ).then_inc(lora_hi, 1)
            first_a(Q01, 0)

            def split_merged():
                for part in range(2):
                    act.wait_ge(weff_ready, 8 * part + 7)
                    for c in range(2):
                        act.activation(wb_hi[:, c, part * 512:part * 512 + 512].rearrange(
                            "p (k o) -> p k o", o=P), gate_tile(c, part), ACT.Copy
                            ).then_inc([merged_hi, wb_hi_done][part], 1)

            def body(pos, gp, first, last):
                for j in range(G):
                    exps(pos, j)
                    if not (first and j == 0):
                        head_out(pos, j - 1, 0 if j in (1, 2) else 1, (j - 1) % 2)
                    if j < 3:
                        take_hi(pos, 5 * j, qT_hi[:, (j + 1) % 2, :])
                    elif not last:
                        take_hi(pos, 15, kT_hi[:], scale=qkw[:, 0:1])
                    if j == 0:
                        act.activation(v_hi[:], raw[KV][:, :, HD:2 * HD], ACT.Copy
                                       ).then_inc(v_hi_done, 1)
                    if first:
                        split_b(*[(1, pos.at(0, 32, 320), gate_used(pos, 1)),
                                  (1, pos.at(0, 48, 320), gate_used(pos, 3)),
                                  (1, pos.at(0, 64, 320), gate_used(pos, 5)),
                                  (0, pos.at(0, 80, 320), out_used(pos, 2))][j])
                        if j < 2:
                            gate_exp_of(pos, 2 + 2 * j)
                            split_b(0, pos.at(0, 48 + 16 * j, 320), gate_used(pos, 2 + 2 * j))
                    elif last:
                        split_b(*[(1, pos.at(32, 48, 64), out_used(pos, -1)),
                                  (0, pos.at(32, 64, 64), out_used(pos, 0)),
                                  (0, pos.at(32, 80, 64), out_used(pos, 1)),
                                  (0, pos.at(32, 96, 64), out_used(pos, 2))][j])
                        if j in (1, 2):
                            gate_exp_of(pos, 5 + j)
                            split_b(1, pos.at(32, 48 + 16 * j, 64), gate_used(pos, 5 + j))
                    else:
                        split_b((j + 1) % 2, pos.at(32, 16 * ((5 + j) // 2 + 1), 64),
                                out_used(pos, j - 1))
                    for tile, t in PROJ[j]:
                        if j == 0 and t == 2:
                            split_a(pos, 3 + KV, gp, (a_done, pos.at(12, 8)))
                        tile += 0 if tile == Q23 else 3
                        if last and tile != Q23:
                            continue
                        if t == 0 and tile % 3 == KV:
                            act.wait_ge(v_ready, pos.at(1, 1))
                        if first and (tile, t) == (Q23, 0):
                            act.wait_ge(fin_done, pos.gate(3))
                        copy_rows(pos, tile, t)
                        turn[0] += 1
                        if t == 3:
                            rsqrt(pos, tile, 4 if tile % 3 == KV else 8)
                    if j == 1:
                        split_a(pos, 3 + Q01, gp, (a_done, pos.at(12, 12)))
                    if j == 3 and last:
                        for c in range(2, NK):
                            take_hi(pos, 15 + c, xn_hi[:, c, :])
                    if not (first and j < 2):
                        turn[0] += 4
                    c = 23 if last and j == 3 else 5 * j + 1
                    for k in range(NT):
                        if k == 3 and j == 3 and not last:
                            take_hi(pos, 19, qT_hi[:, 0, :])
                            c += 1
                        w = slice(PT_AT[k], PT_AT[k] + S - P * k)
                        take_hi(pos, c + k, pT_hi[:, w], slice(P * k, S))
                        if j == 3 and not last and k >= 2:
                            split_a(pos, 3 + Q23, gp, (a_done, pos.at(12, 16)), (k - 2,))
                    if last and j == 2:
                        for c in range(2):
                            take_hi(pos, 15 + c, xn_hi[:, c, :])
                    if first and j < 2:
                        gate_exp_of(pos, 3 + 2 * j)
                    if first and j == 1:
                        act.wait_ge(ln_var, pos.b + 2)
                        act.activation(lnv_x[:], var_x[:], ACT.Ln).then_inc(ln_log, 1)
                        act.wait_ge(ln_log, pos.b + 2)
                        act.activation(rinv_x[:], lnv_x[:], ACT.Exp, scale=-0.5).then_inc(ln_r0, 1)

            act.wait_ge(qkw_ready, 1)
            act.wait_ge(lw_in, 16 * 9)
            def batch(b, opening):
                turn[0] = 0
                pos = Pos(act, b, 0)
                act.wait_ge(fin_done, pos.gate(1))
                for t in range(NT):
                    copy_rows(pos, KV, t)
                    turn[0] += 1
                    if opening and t == 1:
                        first_a(Q01, 1)
                rsqrt(pos, KV, 4)
                if opening:
                    split_merged()
                else:
                    split_b(0, pos.at(0, 16, 320), out_used(pos, 0))
                    split_a(pos, Q23, 0, (a_done, pos.at(12, 4)))
                act.wait_ge(fin_done, pos.gate(2))
                for t in range(NT):
                    copy_rows(pos, Q01, t)
                    turn[0] += 1
                rsqrt(pos, Q01, 8)
                if opening:
                    split_a(pos, Q23, 0, (a_done, pos.at(12, 4)))
                else:
                    split_b(1, pos.at(0, 16, 320), out_used(pos, 1))
                gate_exp_of(pos, 0)
                take_hi(pos, -2, kT_hi[:], scale=qkw[:, 0:1])
                take_hi(pos, -1, qT_hi[:, 0, :])
                split_b(0, pos.at(0, 32, 320), gate_used(pos, 0))
                gate_exp_of(pos, 1)
                body(pos, 0, True, False)
                with act.Fori(0, 3) as pair:
                    for h in range(2):
                        turn[0] = 0
                        body(Pos(act, b, pair * 2 + (1 + h)), (1 + h) % 2, False, False)
                turn[0] = 0
                p = Pos(act, b, 7)
                body(p, 1, False, True)
                head_out(p, 3, 1, 1)
                split_b(1, p.at(32, 96, 64), out_used(p, 3))

            batch(0, True)
            with act.Fori(1, BATCH) as b:
                batch(b, False)

        @block.gpsimd
        def _(pool):
            pool.nop().then_inc(wa_ready, SLOT2)
            pool.nop().then_inc(wb_ready, SLOT2)
            pool.nop().then_inc(fin_done, FIN_LEAD)

            def low_a(pos, tile, parity):
                slot = (parity + tile) % 2
                for half in range(2):
                    w = slice(half * TILE, (half + 1) * TILE)
                    pool.wait_ge(wa_hi_done, pos.at(6, 2 * tile + half + 1))
                    pool.tensor_tensor(wa_lo[:, slot, w], stage_a[:, half, :], wa_hi[:, slot, w],
                                       ALU.subtract).then_inc(wa_ready, 1)

            def low_b(slot, made):
                pool.wait_ge(wb_hi_done, made)
                pool.tensor_tensor(wb_lo[:, slot, :], stage_b[:, slot, :], wb_hi[:, slot, :],
                                   ALU.subtract).then_inc(wb_ready, 1)

            def bias_of(pos, j):
                wait_alone(pool, scored, pos.at(16, 4 * j - 4 + SLOT2))
                pool.tensor_scalar(bias_sb[:, j % 2, :], rel_sb[:], slope[:, j % 4:j % 4 + 1], None,
                                   ALU.mult).then_inc(bias_ready, 1)

            for tile in (KV, Q01):
                for half in range(2):
                    w = slice(half * TILE, (half + 1) * TILE)
                    pool.wait_ge(wa_hi_done, 2 * tile + half + 1)
                    pool.tensor_tensor(wa_lo[:, tile, w], stage_a[:, half, :], wa_hi[:, tile, w],
                                       ALU.subtract).then_inc(wa_ready, 1)
                if tile == KV:
                    pool.wait_ge(const_in, 16 * CONSTS)
                    pool.tensor_scalar(bias_sb[:, 0, :], rel_sb[:], slope[:, 0:1], None, ALU.mult
                                       ).then_inc(bias_ready, 1)

            def low_merged():
                for part in range(2):
                    for c in range(2):
                        pool.wait_ge([merged_hi, wb_hi_done][part], c + 1)
                        w = slice(part * 512, part * 512 + 512)
                        low = pool.tensor_tensor(
                            wb_lo[:, c, w].rearrange("p (k o) -> p k o", o=P), gate_tile(c, part),
                            wb_hi[:, c, w].rearrange("p (k o) -> p k o", o=P), ALU.subtract)
                        if part == 1:
                            low.then_inc(wb_ready, 1)

            def body(pos, gp, first, last):
                for j in range(G):
                    if j == 3:
                        wait_alone(pool, bias_ready, pos.at(4, 4))
                        if last:
                            pool.tensor_copy(slope[:], slope0[:]).then_inc(slope_ready, 1)
                        else:
                            pool.tensor_scalar(slope[:], slope[:], 0.5, None, ALU.mult
                                               ).then_inc(slope_ready, 1)
                        wait_alone(pool, slope_ready, pos.at(1, 1))
                    if first:
                        low_b([1, 1, 1, 0][j], pos.at(0, [4, 6, 8, 9][j], 40))
                    elif last:
                        low_b([1, 0, 0, 0][j], pos.at(4, [6, 7, 9, 11][j], 8))
                    else:
                        low_b((j + 1) % 2, pos.at(4, 6 + j, 8))
                    bias_of(pos, j + 1)
                    if first and j < 2:
                        low_b(0, pos.at(0, [5, 7][j], 40))
                    if last and j in (1, 2):
                        low_b(1, pos.at(4, [8, 10][j - 1], 8))
                    if j == 0:
                        low_a(pos, 3 + KV, gp)
                    if j == 1:
                        low_a(pos, 3 + Q01, gp)
                    if j == 3 and not last:
                        low_a(pos, 3 + Q23, gp)

            def batch(b, opening):
                pos = Pos(pool, b, 0)
                if not opening:
                    low_b(0, pos.at(0, 1, 40))
                if opening:
                    low_merged()
                low_a(pos, Q23, 0)
                if not opening:
                    low_b(1, pos.at(0, 2, 40))
                low_b(0, pos.at(0, 3, 40))
                body(pos, 0, True, False)
                with pool.Fori(0, 3) as pair:
                    for h in range(2):
                        body(Pos(pool, b, pair * 2 + (1 + h)), (1 + h) % 2, False, False)
                p = Pos(pool, b, 7)
                body(p, 1, False, True)
                low_b(1, p.at(4, 12, 8))
                for c in range(NK):
                    pool.wait_ge(fin_step, b * 8 + (c + 1))
                    pool.tensor_tensor(acc[:, c, :], x_at[c], acc[:, c, :], ALU.add
                                       ).then_inc(fin_done, 1)

            batch(0, True)
            with pool.Fori(1, BATCH) as b:
                batch(b, False)

        @block.vector
        def _(dve):
            dve.nop().then_inc(scored, SLOT2)
            dve.nop().then_inc(tr_free, SLOT3)
            dve.nop().then_inc(out_free, SLOT2)
            dve.nop().then_inc(ot_free, 1)
            def newton_step(n, count, done, rinv, var, tmp):
                dve.tensor_tensor(tmp[:, 0:n], rinv[:, 0:n], rinv[:, 0:n], ALU.mult).then_inc(done, 1)
                dve.wait_ge(done, count(1))
                dve.tensor_tensor(tmp[:, 0:n], tmp[:, 0:n], var[:, 0:n], ALU.mult).then_inc(done, 1)
                dve.wait_ge(done, count(2))
                dve.tensor_scalar(tmp[:, 0:n], tmp[:, 0:n], -0.5, 1.5, ALU.mult, ALU.add
                                  ).then_inc(done, 1)
                dve.wait_ge(done, count(3))
                dve.tensor_tensor(rinv[:, 0:n], rinv[:, 0:n], tmp[:, 0:n], ALU.mult).then_inc(done, 1)
                dve.wait_ge(done, count(4))

            def layer_norm_stats(loaded, r, tiles):
                if loaded is not None and 0 in tiles:
                    dve.wait_ge(x_in, loaded)
                for t in tiles:
                    if loaded is None:
                        dve.wait_ge(x0_in[t], 16)
                    for i in range(2):
                        ins = dve.bn_stats(bn[:, t, 6 * i:6 * i + 6], xtok[:, t, 512 * i:512 * i + 512])
                if NT - 1 not in tiles:
                    return
                ins.then_inc(ln_stat, 1)
                wait_alone(dve, ln_stat, r(2, 1))
                for t in range(NT):
                    ins = dve.bn_aggr(mv[:, t, :], bn[:, t, :])
                ins.then_inc(ln_stat, 1)
                dve.wait_ge(ln_stat, r(2, 2))
                dve.tensor_scalar(var_x[:], mv[:, :, 1], LN_EPS, None, ALU.add).then_inc(ln_var, 1)

            def scale_x(r, tiles):
                if 0 in tiles:
                    dve.wait_ge(ln_r0, r(1, 1))
                    newton_step(NT, lambda c: r(4, c), ln_newton, rinv_x, var_x, tmp_x)
                for t in tiles:
                    dve.tensor_scalar(xtok[:, t, :], xtok[:, t, :], mv[:, t, 0:1], rinv_x[:, t:t + 1],
                                      ALU.subtract, ALU.mult).then_inc(ln_ready, 1)

            def row_stats(pos, tile, t):
                heads = 1 if tile % 3 == KV else 2
                dve.wait_ge(a_free, pos.at(12, 4 * tile + t + 1 + 1))
                for h in range(heads):
                    r = raw[tile % 3][:, t, h * HD:h * HD + HD]
                    at = t * heads + h
                    ins = dve.tensor_tensor_reduce(sq[:, at, :], r, r, 1.0, 0.0, ALU.mult, ALU.add,
                                                   ss[:, at:at + 1])
                if t == 3:
                    ins.then_inc(stat_ready, 1)

            def row_var(pos, tile):
                dve.wait_ge(stat_ready, pos.at(3, tile + 1))
                if tile % 3 == KV:
                    dve.tensor_scalar(var[:, 0:4], ss[:, 0:4], 1.0 / HD, RMS_EPS, ALU.mult, ALU.add
                                      ).then_inc(var_ready, 1)
                else:
                    dve.tensor_scalar(var[:], ss[:], HD * RMS_EPS, None, ALU.add
                                      ).then_inc(var_ready, 1)

            def row_factors(pos, tile):
                dve.wait_ge(r0_done, pos.at(3, tile + 1))
                newton_step(4 if tile % 3 == KV else 8, lambda c: pos.at(12, 4 * tile + c),
                            newton, rinv, var, tmp)

            def scale_rows(tile, odd=0):
                r = raw[tile % 3][:, :, odd * HD:odd * HD + HD]
                if tile % 3 == KV:
                    f = rinv[:, 0:NT]
                else:
                    f = rinv[:].rearrange("p (t h) -> p t h", h=2)[:, :, odd]
                dve.tensor_tensor(r, r, f.unsqueeze(2).to_broadcast([P, NT, HD]), ALU.mult
                                  ).then_inc(odd_ready if odd else rows_ready, 1)

            def take_lo(pos, c, dst, hi, src=None, scale=None):
                dve.wait_ge(tr_hi, pos.tb(c) + 1)
                bank = tr_ps[(c + 1) % 3][:]
                bank = bank if src is None else bank[:, src]
                if scale is None:
                    dve.tensor_tensor(dst, bank, hi, ALU.subtract).then_inc(tr_free, 1)
                else:
                    dve.scalar_tensor_tensor(out=dst, in0=bank, scalar=scale, in1=hi, op0=ALU.mult,
                                             op1=ALU.subtract).then_inc(tr_free, 1)

            def bias_and_max(pos, j, c=None):
                if c is not None:
                    gate_sum(pos, c)
                dve.wait_ge(bias_ready, pos.at(4, j + 1))
                for i in range(NT):
                    if c is not None and i >= 2:
                        gate_inverse(pos, c, i - 2)
                    if j == 0 and i == 2:
                        scale_rows(Q01, 1)
                    if j == 1 and i >= 2:
                        scale_rows(Q23, i - 2)
                    w = P * (i + 1)
                    wait_alone(dve, s_done, pos.at(16, 4 * j + i + 1))
                    dve.tensor_tensor_reduce(prob[:, P_AT[i]:P_AT[i] + w], sc_ps[i % 2][:, 0:w],
                                             bias_sb[:, j % 2, S - w:S], -1.0, 3e38,
                                             ALU.add, ALU.min, negmax[:, i:i + 1]).then_inc(scored, 1)

            def normalise(pos, j):
                dve.wait_ge(exp_done, pos.at(16, 4 * j + 4))
                dve.reciprocal(rs_inv[:], rowsum[:]).then_inc(rs_ready, 1)
                dve.wait_ge(rs_ready, pos.at(4, j + 1))
                for i in range(NT):
                    p = prob[:, P_AT[i]:P_AT[i] + P * (i + 1)]
                    ins = dve.tensor_scalar(p, p, rs_inv[:, i:i + 1], None, ALU.mult)
                ins.then_inc(prob_ready, 1)

            def head_out(pos, j, pair, hh):
                dve.wait_ge(ot_hi, pos.at(4, j + 1))
                dve.tensor_tensor(o_lo[:, pair, hh, :], ot_ps[:], o_hi[:, pair, hh, :], ALU.subtract
                                  ).then_inc(ot_free, 1)

            def add_out(pos, j, c, chunk, copy):
                bank = proj_ps[turn[0] % 2][:]
                turn[0] += 1
                dve.wait_ge(out_done, pos.out(j, c + 1 + OUT_LEAD))
                a = acc[:, chunk, :]
                if copy:
                    dve.tensor_copy(a, bank).then_inc(out_free, 1)
                else:
                    dve.tensor_tensor(a, a, bank, ALU.add).then_inc(out_free, 1)

            def gate_sum(pos, c):
                e = g_buf[:, c % 2, :]
                dve.wait_ge(gate_exp, pos.gate(c + 1))
                dve.tensor_scalar(e, e, 1.0, None, ALU.add).then_inc(gate_step, 1)

            def gate_inverse(pos, c, quarter):
                e = g_buf[:, c % 2, quarter * P:(quarter + 1) * P]
                if quarter == 0:
                    dve.wait_ge(gate_step, pos.at(0, 2 * c + 1, 16))
                ins = dve.reciprocal(e, e)
                if quarter == 3:
                    ins.then_inc(gate_step, 1)

            def gate_product(pos, c):
                z = x_buf[:, c % 2, :]
                dve.wait_ge(gate_step, pos.at(0, 2 * c + 2, 16))
                dve.tensor_tensor(z, z, g_buf[:, c % 2, :], ALU.mult).then_inc(gate_ready, 1)

            def gate(pos, c, parts=(0, 1, 2, 3)):
                for quarter in parts:
                    if quarter == 0:
                        gate_sum(pos, c)
                    gate_inverse(pos, c, quarter)
                    if quarter == 3:
                        gate_product(pos, c)

            GATE_START = [(1, (0, 1, 2, 3)), (3, (0, 1, 2, 3)), (4, (0, 1)), None]
            GATE_PARTS = [[None, (2, (0,)), (2, (1, 2)), (2, (3,))],
                          [None, None, None],
                          [None, (4, (2,)), None],
                          [(4, (3,)), None]]
            GATE_PARTS7 = [(5, (0,)), (5, (1,)), (5, (2,)), (5, (3,))]
            STAT_TILES = {(1, 0): (0, 1), (1, 1): (2,), (1, 2): (3,)}

            def first_lo(t):
                for half in range(2):
                    c = 2 * t + half
                    dve.wait_ge(tr_hi, c + 1)
                    x = slice(4 * half, 4 * half + 4)
                    dve.tensor_tensor(xn_lo[:, x, t * P:t * P + P],
                                      tr_ps[c % 3][:].rearrange("p (k o) -> p k o", o=P),
                                      xn_hi[:, x, t * P:t * P + P], ALU.subtract
                                      ).then_inc(tr_free, 1)

            layer_norm_stats(None, lambda k, c: c, range(NT))
            for t in range(NT):
                scale_x(lambda k, c: c, (t,))
                if t > 0:
                    first_lo(t - 1)
            first_lo(NT - 1)
            dve.wait_ge(const_in, 16 * CONSTS)
            dve.tensor_tensor(qkw[:], qw_sb[:], kw_sb[:], ALU.mult).then_inc(qkw_ready, 1)
            dve.wait_ge(b_in[1], 16)
            dve.wait_ge(lw_in, 16 * 9)
            dve.tensor_scalar(stage_b[:, 1, :], stage_b[:, 1, :], lw_sb[:, 0:1], LORA_SCALE,
                              ALU.mult, ALU.mult).then_inc(lora_scaled, 1)
            for i in range(2):
                dve.wait_ge(lora_hi, i + 1)
                dve.tensor_tensor(o_lo[:, i].rearrange("p h s -> p (h s)"), stage_b[:, i, :],
                                  o_hi[:, i].rearrange("p h s -> p (h s)"), ALU.subtract
                                  ).then_inc(lora_ready, 2)

            def merge_gate():
                for n in range(2 * NK):
                    k, half = divmod(n, 2)
                    dve.wait_ge(wt_in[k], 16)
                    dve.wait_ge(weff_done, n + 1)
                    w = gate_rows(k)[:, half * 512:half * 512 + 512]
                    dve.tensor_tensor(w, w, merge_ps[n % 3][:], ALU.add).then_inc(weff_ready, 1)

            turn = [0]

            def body(pos, gp, first, last):
                for j in range(G):
                    bias_and_max(pos, j, 7 if last and j == 3 else None)
                    if last and j == 3:
                        gate_inverse(pos, 7, 2)
                    if first and j == 0:
                        gate(pos, 0, (2, 3))
                    normalise(pos, j)
                    if not (first and j == 0):
                        head_out(pos, j - 1, 0 if j in (1, 2) else 1, (j - 1) % 2)
                    if j < 3:
                        take_lo(pos, 5 * j, qT_lo[:, (j + 1) % 2, :], qT_hi[:, (j + 1) % 2, :])
                    elif not last:
                        take_lo(pos, 15, kT_lo[:], kT_hi[:], scale=qkw[:, 0:1])
                    if j == 0:
                        dve.wait_ge(v_hi_done, pos.at(1, 1))
                        dve.tensor_tensor(v_lo[:], raw[KV][:, :, HD:2 * HD], v_hi[:], ALU.subtract
                                          ).then_inc(v_ready, 1)
                    if first and GATE_START[j]:
                        gate(pos, *GATE_START[j])
                    if first and j < 2:
                        turn[0] += 1
                    if last and j in (1, 2):
                        turn[0] += 1
                    if last and j == 2:
                        gate(pos, 6)
                    if last and j == 1:
                        scale_x(lambda k, c: pos.b * k + (k + c), range(NT))
                    groups = [(tile if tile == Q23 else tile + 3, t) for tile, t in PROJ[j]
                              if tile == Q23 or not last]
                    ended = None
                    for tile, t in groups:
                        row_stats(pos, tile, t)
                        turn[0] += 1
                        at = groups.index((tile, t))
                        if first and GATE_PARTS[j][at]:
                            gate(pos, *GATE_PARTS[j][at])
                        if last and j == 0:
                            gate(pos, *GATE_PARTS7[at])
                        if first and (j, at) in STAT_TILES:
                            layer_norm_stats(pos.b * 16 + 16, lambda k, c: pos.b * k + (k + c),
                                             STAT_TILES[j, at])
                        if t == 3:
                            row_var(pos, tile)
                            if (tile, t) != groups[-1]:
                                row_factors(pos, tile)
                                scale_rows(tile)
                            else:
                                ended = tile
                    if first and j == 2:
                        for i in range(2):
                            dve.wait_ge(res_out[i], pos.at(0, 16, 64))
                    adds = not (first and j < 2)
                    half = 4 * (j % 2)
                    if last and j == 3:
                        def x_lo(chunks):
                            for c in chunks:
                                take_lo(pos, 15 + c, xn_lo[:, c, :], xn_hi[:, c, :])

                        def prob_lo(k):
                            w = slice(PT_AT[k], PT_AT[k] + S - P * k)
                            take_lo(pos, 23 + k, pT_lo[:, w], pT_hi[:, w], slice(P * k, S))

                        x_lo((2, 3, 4))
                        add_out(pos, j, 0, half, False)
                        x_lo((5, 6, 7))
                        add_out(pos, j, 1, half + 1, False)
                        for k in range(3):
                            prob_lo(k)
                        add_out(pos, j, 2, half + 2, False)
                        prob_lo(3)
                        gate(pos, 7, (3,))
                        continue
                    if adds:
                        add_out(pos, j, 0, half, first)
                    if ended is not None:
                        row_factors(pos, ended)
                    if j == 3 and ended is not None:
                        scale_rows(ended)
                    elif adds:
                        add_out(pos, j, 1, half + 1, first)
                    c = 23 if last and j == 3 else 5 * j + 1
                    for k in range(NT):
                        if k == 3:
                            if adds:
                                add_out(pos, j, 2, half + 2, first)
                            if j == 3 and not last:
                                take_lo(pos, 19, qT_lo[:, 0, :], qT_hi[:, 0, :])
                                c += 1
                        w = slice(PT_AT[k], PT_AT[k] + S - P * k)
                        take_lo(pos, c + k, pT_lo[:, w], pT_hi[:, w], slice(P * k, S))
                        if k == 1 and j == 3 and ended is not None:
                            add_out(pos, j, 1, half + 1, first)
                    if last and j == 2:
                        for c in range(2):
                            take_lo(pos, 15 + c, xn_lo[:, c, :], xn_hi[:, c, :])
                    if adds:
                        add_out(pos, j, 3, half + 3, first)
                    else:
                        turn[0] += 1

            def batch(b, opening):
                turn[0] = 0
                pos = Pos(dve, b, 0)
                for tile in (KV, Q01):
                    for t in range(NT):
                        row_stats(pos, tile, t)
                        turn[0] += 1
                    row_var(pos, tile)
                    row_factors(pos, tile)
                    scale_rows(tile)
                    if opening and tile == KV:
                        merge_gate()
                turn[0] += 2
                take_lo(pos, -2, kT_lo[:], kT_hi[:], scale=qkw[:, 0:1])
                take_lo(pos, -1, qT_lo[:, 0, :], qT_hi[:, 0, :])
                gate(pos, 0, (0, 1))
                body(pos, 0, True, False)
                with dve.Fori(0, 3) as pair:
                    for h in range(2):
                        turn[0] = 0
                        body(Pos(dve, b, pair * 2 + (1 + h)), (1 + h) % 2, False, False)
                turn[0] = 0
                p = Pos(dve, b, 7)
                body(p, 1, False, True)
                head_out(p, 3, 1, 1)
                add_out(p, 3, 3, 7, False)
                for c in range(NK + 1):
                    if c < NK:
                        add_out(p, 4, c, c, False)
                    if c > 0:
                        done = c - 1
                        dve.wait_ge(out_free, p.out(4, done + 1 + SLOT2))
                        loads = 16 if done == NK - 1 else 32
                        dve.wait_ge(fin_in[done], b * loads + loads)
                        a = acc[:, done, :]
                        dve.tensor_tensor(a, a, gate_at[done], ALU.mult).then_inc(fin_step, 1)

            batch(0, True)
            with dve.Fori(1, BATCH) as b:
                batch(b, False)


def kernel(**inputs):
    import numpy as np
    import concourse.bacc as bacc
    from concourse.bass_utils import run_bass_kernel_spmd

    def f(name):
        return np.asarray(inputs[name])

    x = f("L0_attn_x")
    x_tok = x.reshape(BATCH, NT, P, D).transpose(0, 2, 1, 3)
    wq = f("L0_attn_Wq").T.reshape(2, 4, P, HKV, 2, 256)
    wk = f("L0_attn_Wk").T.reshape(2, 4, P, HKV, 1, HD)
    wv = f("L0_attn_Wv").T.reshape(2, 4, P, HKV, 1, HD)
    wkv = np.concatenate([wk, wv], axis=-1)
    wa = np.concatenate([wkv, wq], axis=4).transpose(3, 4, 0, 2, 1, 5).reshape(HKV * 6, P, TILE)
    wo = f("L0_attn_Wo").T.reshape(HKV, 2, 2, HD, 2, 512).transpose(0, 1, 4, 3, 2, 5)
    key = np.arange(S)[None, :] - np.arange(P)[:, None] - (S - P)
    start = 2.0 ** (-2.0 ** (-2.0))
    arrays = {
        "x_tok": np.roll(x_tok, -1, axis=0),
        "x_first": x_tok[0],
        "xT": x.transpose(0, 2, 1).reshape(BATCH * NK, P, S),
        "wa": wa,
        "wo": wo.reshape(HKV * 4, P, TILE),
        "wT": f("L0_ffn_W").T.reshape(NK, P, D),
        "lora_a": f("L0_ffn_lora_A").reshape(P, D),
        "lora_bt": f("L0_ffn_lora_B").transpose(0, 2, 1).reshape(P, D),
        "lw": f("L0_ffn_lora_weights").reshape(8, 1),
        "ffn_b": f("L0_ffn_bias").reshape(NK, P).T,
        "qw": f("L0_attn_q_norm_w").reshape(P, 1),
        "kw": f("L0_attn_k_norm_w").reshape(P, 1),
        "rel": np.where(key > 0, MASKED, key).astype(np.float32),
        "slopes": np.tile(np.array([start * start ** i for i in range(G)], np.float32), (P, 1)),
        "ident": np.eye(P, dtype=np.float32),
    }
    arrays = {k: np.ascontiguousarray(v) for k, v in arrays.items()}
    nc = bacc.Bacc("TRN2", target_bir_lowering=False, num_devices=1)
    args = [nc.dram_tensor(k, v.shape, F32, kind="ExternalInput").ap() for k, v in arrays.items()]
    outT = nc.dram_tensor("outT", (BATCH * NK, P, S), F32, kind="ExternalOutput").ap()
    build_layer(nc, *args, outT)
    got = run_bass_kernel_spmd(nc, [arrays], core_ids=[0]).results[0]["outT"]
    return np.ascontiguousarray(got.reshape(BATCH, D, S).transpose(0, 2, 1))
```
